# Optimizing a Trainium2 kernel written in Bass

```python
import numpy as np
import jax
import jax.numpy as jnp

def _softmax(x, axis=-1):
    return jax.nn.softmax(x, axis=axis)

def _gelu(x):
    return jax.nn.gelu(x, approximate=True)

def _silu(x):
    return jax.nn.silu(x)

def _sigmoid(x):
    return jax.nn.sigmoid(x)

def _layernorm(x, axis=-1, eps=1e-05):
    m = jnp.mean(x, axis=axis, keepdims=True)
    v = jnp.var(x, axis=axis, keepdims=True)
    return (x - m) / jnp.sqrt(v + eps)

def _scatter_add(tgt, idx, src, axis=0):
    return tgt.at[idx].add(src)

def _segment_sum(src, seg, n):
    return jax.ops.segment_sum(src, seg, n)
kernel_name = 'mk_early_fusion_d2_tok_img768_r4_4da883'

def setup_inputs(seed: int=0):
    np.random.seed(seed)
    _w = jnp.asarray

    def _rec_inputs():
        import jax
        import jax.numpy as jnp
        _rk = jax.random.key(seed)
        x = -0.00016672 + 0.999947 * jax.random.normal(jax.random.fold_in(_rk, 1), (32, 3, 96, 96), jnp.float32)
        txt = 0.000941618 + 1.41341 * jax.random.normal(jax.random.fold_in(_rk, 2), (32, 128, 192), jnp.float32)
        return (x, txt)
    x, txt = _rec_inputs()

    def _L0_tok_setup():
        import jax, jax.numpy as jnp
        import numpy as np
        PATCH = 16

        def _patchify(x):
            B, C, H, Wd = x.shape
            p = PATCH
            Hp, Wp = (H // p, Wd // p)
            x = x.reshape(B, C, Hp, p, Wp, p)
            x = x.transpose(0, 2, 4, 1, 3, 5)
            return x.reshape(B, Hp * Wp, C * p * p)
        key = jax.random.key(seed)
        k1, k2, k3, k4 = jax.random.split(key, 4)
        B, C, H, W_ = (64, 3, 96, 96)
        embed_dim = 192
        patch_dim = C * PATCH * PATCH
        num_patches = H // PATCH * (W_ // PATCH)
        x = jax.random.normal(k1, (B, C, H, W_), dtype=jnp.float32)
        W = jax.random.normal(k2, (embed_dim, patch_dim), dtype=jnp.float32) * (1.0 / np.sqrt(patch_dim))
        b = jax.random.normal(k3, (embed_dim,), dtype=jnp.float32) * 0.01
        pos_embed = jax.random.normal(k4, (1, num_patches, embed_dim), dtype=jnp.float32)
        return {'x': x, 'W': W, 'b': b, 'pos_embed': pos_embed}
    _L0_tok_all = _L0_tok_setup()
    _L0_tok_in = {k: v for k, v in _L0_tok_all.items() if k in ('W', 'b', 'pos_embed')}
    del _L0_tok_all

    def _L0_attn_setup():
        import jax, jax.numpy as jnp
        import numpy as np
        B, T, D = (2, 1024, 192)
        H, HD = (6, D // 6)
        key = jax.random.key(seed)
        ks = jax.random.split(key, 8)
        s = 0.02
        return {'x': jax.random.normal(ks[0], (B, T, D), dtype=jnp.float32), 'Wq': jax.random.normal(ks[1], (D, D), dtype=jnp.float32) * s, 'Wk': jax.random.normal(ks[2], (D, D), dtype=jnp.float32) * s, 'Wv': jax.random.normal(ks[3], (D, D), dtype=jnp.float32) * s, 'Wo': jax.random.normal(ks[4], (D, D), dtype=jnp.float32) * s, 'anchor_w': jax.random.normal(ks[5], (H, HD, 6), dtype=jnp.float32) * s, 'anchors': jnp.sign(jax.random.normal(ks[6], (H, 6), dtype=jnp.float32)), 'lam': jnp.full((H,), 0.1, dtype=jnp.float32)}
    _L0_attn_all = _L0_attn_setup()
    _L0_attn_in = {k: v for k, v in _L0_attn_all.items() if k in ('Wq', 'Wk', 'Wv', 'Wo', 'anchor_w', 'anchors', 'lam')}
    del _L0_attn_all

    def _L0_ffn_setup():
        import jax, jax.numpy as jnp
        import numpy as np
        B, S, D_IN, D_HID, D_OUT = (32, 128, 192, 768, 192)
        key = jax.random.key(seed)
        k1, k2, k3, k4 = jax.random.split(key, 4)
        init_k = float(np.sqrt(1.0 / D_IN))
        init_k2 = float(np.sqrt(1.0 / D_HID))
        x = jax.random.normal(k1, (B, S, D_IN), dtype=jnp.float32)
        in_weight = jax.random.uniform(k2, (D_HID, D_IN), dtype=jnp.float32, minval=-init_k, maxval=init_k)
        in_bias = jax.random.uniform(k3, (D_HID,), dtype=jnp.float32, minval=-init_k, maxval=init_k)
        out_weight = jax.random.uniform(k4, (D_HID, D_OUT), dtype=jnp.float32, minval=-init_k2, maxval=init_k2)
        return {'x': x, 'in_weight': in_weight, 'in_bias': in_bias, 'out_weight': out_weight}
    _L0_ffn_all = _L0_ffn_setup()
    _L0_ffn_in = {k: v for k, v in _L0_ffn_all.items() if k in ('in_weight', 'in_bias', 'out_weight')}
    del _L0_ffn_all

    def _L1_attn_setup():
        import jax, jax.numpy as jnp
        import numpy as np
        B, T, C, NH = (8, 256, 192, 12)
        HD = C // NH
        key = jax.random.key(seed)
        k1, k2, k3, k4, k5 = jax.random.split(key, 5)
        s = 0.02
        return {'x': jax.random.normal(k1, (B, T, C), dtype=jnp.float32), 'w_attn': jax.random.normal(k2, (C, 3 * C), dtype=jnp.float32) * s, 'b_attn': jax.random.normal(k3, (3 * C,), dtype=jnp.float32) * s, 'w_proj': jax.random.normal(k4, (C, C), dtype=jnp.float32) * s, 'b_proj': jax.random.normal(k5, (C,), dtype=jnp.float32) * s}
    _L1_attn_all = _L1_attn_setup()
    _L1_attn_in = {k: v for k, v in _L1_attn_all.items() if k in ('w_attn', 'b_attn', 'w_proj', 'b_proj')}
    del _L1_attn_all

    def _L1_ffn_setup():
        import jax, jax.numpy as jnp
        import numpy as np
        NUM_EXPERTS = 8
        TOP_K = 2
        CAPACITY_FACTOR = 1.25
        MAX_GROUP_SIZE = 1024
        MIN_EXPERT_CAPACITY = 4

        def _moe_forward(x, w_router, wi, wo):
            B, T, D = x.shape
            E = NUM_EXPERTS
            num_tokens = B * T
            G = max(num_tokens // MAX_GROUP_SIZE, E)
            while num_tokens % G != 0 or G % E != 0:
                G += 1
            S = num_tokens // G
            C = max(int(TOP_K * CAPACITY_FACTOR * S / E), MIN_EXPERT_CAPACITY)
            xg = x.reshape(G, S, D)
            logits = jnp.einsum('gsd,de->gse', xg.astype(jnp.float32), w_router.astype(jnp.float32))
            probs = jax.nn.softmax(logits, axis=-1)
            gate, idx = jax.lax.top_k(probs, TOP_K)
            idx_kf = jnp.swapaxes(idx, 1, 2).reshape(G, TOP_K * S)
            mask = jax.nn.one_hot(idx_kf, E, dtype=jnp.int32)
            prio = jnp.cumsum(mask, axis=1) * mask - 1
            prio = jnp.swapaxes(prio.reshape(G, TOP_K, S, E), 1, 2)
            prio_se = prio.max(axis=2)
            gate_se = jnp.einsum('gsk,gske->gse', gate, jax.nn.one_hot(idx, E, dtype=gate.dtype))
            dispatch = jax.nn.one_hot(prio_se, C, dtype=x.dtype)
            combine = dispatch * gate_se[..., None].astype(x.dtype)
            expert_in = jnp.einsum('gsec,gsd->egcd', dispatch, xg)
            h = jax.nn.relu(jnp.einsum('egcd,edf->egcf', expert_in, wi))
            expert_out = jnp.einsum('egcf,efd->egcd', h, wo)
            out = jnp.einsum('gsec,egcd->gsd', combine, expert_out)
            return out.reshape(B, T, D)
        key = jax.random.key(seed)
        k1, k2, k3, k4 = jax.random.split(key, 4)
        B, T, D, F = (8, 256, 192, 768)
        x = jax.random.normal(k1, (B, T, D), jnp.float32)
        w_router = jax.random.normal(k2, (D, NUM_EXPERTS), jnp.float32) * D ** (-0.5)
        wi = jax.random.normal(k3, (NUM_EXPERTS, D, F), jnp.float32) * D ** (-0.5)
        wo = jax.random.normal(k4, (NUM_EXPERTS, F, D), jnp.float32) * F ** (-0.5)
        return {'x': x, 'w_router': w_router, 'wi': wi, 'wo': wo}
    _L1_ffn_all = _L1_ffn_setup()
    _L1_ffn_in = {k: v for k, v in _L1_ffn_all.items() if k in ('w_router', 'wi', 'wo')}
    del _L1_ffn_all
    return {'x': x, 'txt': txt, 'L0_tok_W': _L0_tok_in['W'], 'L0_tok_b': _L0_tok_in['b'], 'L0_tok_pos_embed': _L0_tok_in['pos_embed'], 'L0_attn_Wq': _L0_attn_in['Wq'], 'L0_attn_Wk': _L0_attn_in['Wk'], 'L0_attn_Wv': _L0_attn_in['Wv'], 'L0_attn_Wo': _L0_attn_in['Wo'], 'L0_attn_anchor_w': _L0_attn_in['anchor_w'], 'L0_attn_anchors': _L0_attn_in['anchors'], 'L0_attn_lam': _L0_attn_in['lam'], 'L0_ffn_in_weight': _L0_ffn_in['in_weight'], 'L0_ffn_in_bias': _L0_ffn_in['in_bias'], 'L0_ffn_out_weight': _L0_ffn_in['out_weight'], 'L1_attn_w_attn': _L1_attn_in['w_attn'], 'L1_attn_b_attn': _L1_attn_in['b_attn'], 'L1_attn_w_proj': _L1_attn_in['w_proj'], 'L1_attn_b_proj': _L1_attn_in['b_proj'], 'L1_ffn_w_router': _L1_ffn_in['w_router'], 'L1_ffn_wi': _L1_ffn_in['wi'], 'L1_ffn_wo': _L1_ffn_in['wo']}

def reference(x, txt, L0_tok_W, L0_tok_b, L0_tok_pos_embed, L0_attn_Wq, L0_attn_Wk, L0_attn_Wv, L0_attn_Wo, L0_attn_anchor_w, L0_attn_anchors, L0_attn_lam, L0_ffn_in_weight, L0_ffn_in_bias, L0_ffn_out_weight, L1_attn_w_attn, L1_attn_b_attn, L1_attn_w_proj, L1_attn_b_proj, L1_ffn_w_router, L1_ffn_wi, L1_ffn_wo):
    import jax
    import jax.numpy as jnp

    def _L0_tok_ref(x, W, b, pos_embed):
        import jax, jax.numpy as jnp
        import numpy as np
        PATCH = 16

        def _patchify(x):
            B, C, H, Wd = x.shape
            p = PATCH
            Hp, Wp = (H // p, Wd // p)
            x = x.reshape(B, C, Hp, p, Wp, p)
            x = x.transpose(0, 2, 4, 1, 3, 5)
            return x.reshape(B, Hp * Wp, C * p * p)
        patches = _patchify(x)
        tokens = jnp.einsum('bnd,ed->bne', patches, W) + b
        return tokens + pos_embed

    def _L0_attn_ref(x, Wq, Wk, Wv, Wo, anchor_w, anchors, lam):
        import jax, jax.numpy as jnp
        import numpy as np
        B, T, D = (2, 1024, 192)
        H, HD = (6, D // 6)
        b, t, d = x.shape
        scale = HD ** (-0.5)
        q = (x @ Wq.T).reshape(b, t, H, HD).transpose(0, 2, 1, 3)
        k = (x @ Wk.T).reshape(b, t, H, HD).transpose(0, 2, 1, 3)
        v = (x @ Wv.T).reshape(b, t, H, HD).transpose(0, 2, 1, 3)
        scores = jnp.einsum('bhqd,bhkd->bhqk', q, k) * scale
        anchor_h = jnp.einsum('hde,he->hd', anchor_w, anchors)
        anchor_sim = jnp.einsum('bhtd,hd->bht', q, anchor_h)
        scores = scores + (lam[None, :, None] * anchor_sim)[..., None]
        attn = jax.nn.softmax(scores, axis=-1)
        out = jnp.einsum('bhqk,bhkd->bhqd', attn, v)
        out = out.transpose(0, 2, 1, 3).reshape(b, t, d)
        return out @ Wo.T

    def _L0_ffn_ref(x, in_weight, in_bias, out_weight):
        import jax, jax.numpy as jnp
        import numpy as np
        B, S, D_IN, D_HID, D_OUT = (32, 128, 192, 768, 192)
        lead = x.shape[:-1]
        xt = x.reshape(-1, in_weight.shape[1])
        h = jax.nn.gelu(jnp.einsum('td,hd->th', xt, in_weight) + in_bias, approximate=False)
        out = jnp.einsum('th,ho->to', h, out_weight)
        return out.reshape(*lead, out_weight.shape[1])

    def _L1_attn_ref(x, w_attn, b_attn, w_proj, b_proj):
        import jax, jax.numpy as jnp
        import numpy as np
        B, T, C, NH = (8, 256, 192, 12)
        HD = C // NH
        Bv, Tv, Cv = x.shape
        qkv = jnp.einsum('btc,cd->btd', x, w_attn) + b_attn
        q, k, v = jnp.split(qkv, 3, axis=-1)
        q = q.reshape(Bv, Tv, NH, HD).transpose(0, 2, 1, 3)
        k = k.reshape(Bv, Tv, NH, HD).transpose(0, 2, 1, 3)
        v = v.reshape(Bv, Tv, NH, HD).transpose(0, 2, 1, 3)
        scale = 1.0 / np.sqrt(HD).astype(np.float32)
        att = jnp.einsum('bhqd,bhkd->bhqk', q, k) * scale
        causal = jnp.tril(jnp.ones((Tv, Tv), dtype=bool))
        att = jnp.where(causal, att, -jnp.inf)
        att = jax.nn.softmax(att, axis=-1)
        y = jnp.einsum('bhqk,bhkd->bhqd', att, v)
        y = y.transpose(0, 2, 1, 3).reshape(Bv, Tv, Cv)
        return jnp.einsum('btc,cd->btd', y, w_proj) + b_proj

    def _L1_ffn_ref(x, w_router, wi, wo):
        import jax, jax.numpy as jnp
        import numpy as np
        NUM_EXPERTS = 8
        TOP_K = 2
        CAPACITY_FACTOR = 1.25
        MAX_GROUP_SIZE = 1024
        MIN_EXPERT_CAPACITY = 4

        def _moe_forward(x, w_router, wi, wo):
            B, T, D = x.shape
            E = NUM_EXPERTS
            num_tokens = B * T
            G = max(num_tokens // MAX_GROUP_SIZE, E)
            while num_tokens % G != 0 or G % E != 0:
                G += 1
            S = num_tokens // G
            C = max(int(TOP_K * CAPACITY_FACTOR * S / E), MIN_EXPERT_CAPACITY)
            xg = x.reshape(G, S, D)
            logits = jnp.einsum('gsd,de->gse', xg.astype(jnp.float32), w_router.astype(jnp.float32))
            probs = jax.nn.softmax(logits, axis=-1)
            gate, idx = jax.lax.top_k(probs, TOP_K)
            idx_kf = jnp.swapaxes(idx, 1, 2).reshape(G, TOP_K * S)
            mask = jax.nn.one_hot(idx_kf, E, dtype=jnp.int32)
            prio = jnp.cumsum(mask, axis=1) * mask - 1
            prio = jnp.swapaxes(prio.reshape(G, TOP_K, S, E), 1, 2)
            prio_se = prio.max(axis=2)
            gate_se = jnp.einsum('gsk,gske->gse', gate, jax.nn.one_hot(idx, E, dtype=gate.dtype))
            dispatch = jax.nn.one_hot(prio_se, C, dtype=x.dtype)
            combine = dispatch * gate_se[..., None].astype(x.dtype)
            expert_in = jnp.einsum('gsec,gsd->egcd', dispatch, xg)
            h = jax.nn.relu(jnp.einsum('egcd,edf->egcf', expert_in, wi))
            expert_out = jnp.einsum('egcf,efd->egcd', h, wo)
            out = jnp.einsum('gsec,egcd->gsd', combine, expert_out)
            return out.reshape(B, T, D)
        return _moe_forward(x, w_router, wi, wo)
    h = _L0_tok_ref(x, L0_tok_W, L0_tok_b, L0_tok_pos_embed)
    h = jnp.concatenate([h, txt], axis=1)
    h = h + _L0_attn_ref(_layernorm(h, axis=-1), L0_attn_Wq, L0_attn_Wk, L0_attn_Wv, L0_attn_Wo, L0_attn_anchor_w, L0_attn_anchors, L0_attn_lam)
    h = h + _L0_ffn_ref(_layernorm(h, axis=-1), L0_ffn_in_weight, L0_ffn_in_bias, L0_ffn_out_weight)
    h = h + _L1_attn_ref(_layernorm(h, axis=-1), L1_attn_w_attn, L1_attn_b_attn, L1_attn_w_proj, L1_attn_b_proj)
    h = h + _L1_ffn_ref(_layernorm(h, axis=-1), L1_ffn_w_router, L1_ffn_wi, L1_ffn_wo)
    return h

_drawn_inputs = setup_inputs


def setup_inputs(seed=0):
    import zlib

    import numpy as np

    out = dict(_drawn_inputs(seed))
    spreads = {'L0_attn_lam': (0.10000000149011612, 0.6)}
    factors = {'L0_tok_b': 8.0,
     'L0_attn_Wq': 8.0,
     'L0_attn_Wk': 8.0,
     'L0_attn_Wv': 6.263,
     'L0_attn_Wo': 6.565,
     'L0_attn_anchor_w': 8.0,
     'L0_attn_anchors': 8.0,
     'L0_ffn_in_bias': 3.458,
     'L1_attn_w_attn': 4.059,
     'L1_attn_b_attn': 6.57,
     'L1_attn_w_proj': 3.493,
     'L1_attn_b_proj': 3.186}
    for name, (base, spread) in spreads.items():
        noise = np.random.default_rng([zlib.crc32(name.encode()), seed]).standard_normal(out[name].shape)
        drawn = base * np.exp(spread * noise) if base else spread * noise
        out[name] = jnp.asarray(drawn.astype(out[name].dtype))
    for name, factor in factors.items():
        out[name] = (out[name] * factor).astype(out[name].dtype)
    return out
```

```python
import concourse.bass as bass
from concourse import mybir

F32 = mybir.dt.float32
BF16 = mybir.dt.bfloat16
U32 = mybir.dt.uint32
ALU = mybir.AluOpType
ACT = mybir.ActivationFunctionType
AX = mybir.AxisListType

B, NPATCH, NTXT, D = 32, 36, 128, 192
T = NPATCH + NTXT
HT = T // 2
NT = 2 * B
DH = D // 2
PATCH_DIM = 768
PK = PATCH_DIM // 128
F = 768
FM = F // 128
H0, HD0 = 6, 32
H1, HD1 = 12, 16
EPS = 1e-5
E, TOPK = 8, 2
G = 8
GT = NT // G
S = GT * HT
CAP = int(TOPK * 1.25 * S / E)
CT = (CAP + 1) // 2
SLOTS = 2 * CT
GROUP_SLOTS = E * SLOTS
ALL_SLOTS = G * GROUP_SLOTS
BIG = 1.0e6
MASKED = -1.0e30
ARENA = 36900
PB = 3 * NPATCH
N_WEIGHTS = 19
NPT = -(-B // 3)

C_IDENT = 0
C_ONES = 128
C_QM0 = 256
C_QM1 = C_QM0 + 3
C_MASK_A = 272
C_MASK_B = C_MASK_A + 492
C_TRI = C_MASK_B + 492
C_REV = C_TRI + HT
C_RESET = C_REV + E
C_BASE = C_RESET + 1024
C_HALF = C_BASE + 128
C_ALL = C_HALF + 8

USES = []
P0_ORDER = (0, 2, 1, 3)
P1_ORDER = (0, 1, 4, 5, 2, 3)


def _uses():
    ring = {"scores": [0, 1, 2], "probs": [3, 4]}
    seen = dict.fromkeys(ring, 0)

    def use(layer, kind, *names):
        for name in names:
            banks = ring[kind]
            USES.append((name, layer, banks[seen[kind] % len(banks)]))
            seen[kind] += 1

    use(0, "scores", *[f"scores0_{u}" for u in range(4)])
    use(1, "scores", *[f"scores1_{u}" for u in range(6)])
    use(0, "probs", *[f"probs0T_{u}" for u in P0_ORDER])
    use(1, "probs", *[f"probs1T_{u}" for u in P1_ORDER])
    USES.extend([("x3T", 1, 5), ("q1", 1, 6), ("k1", 1, 7), ("v1", 1, 5), ("att0", 0, 6), ("x1T", 0, 7),
                 ("proj0", 0, 5), ("att1", 1, 6), ("v0", 0, 7), ("x2T", 0, 5), ("q0", 0, 7), ("proj1", 1, 5),
                 ("hid_a", 0, 6), ("hid_b", 0, 7), ("ffn", 0, 5), ("x4T", 1, 6), ("k0", 0, 7), ("logits", 1, 6)])


_uses()
PLACE = {name: n for n, (name, _, _) in enumerate(USES)}
AHEAD = ("x1T", "v0", "q0", "k0")


def rounds(name, i, back=0):
    layer = USES[PLACE[name]][1]
    if name in AHEAD:
        return i + 2 - back
    return i + (1 - layer) - back


def program(nc, patchesT, txt, tok_w, tok_bias, tok_b, wq, wk, wv, wo, anchor_w, anchors, lam,
            ffn_in, ffn_bias, ffn_out, w_attn, qk_bias, v_bias, w_proj, proj_bias,
            w_router, wi, wo_moe, consts, out):
    nsem = [0]

    def sem(name):
        nsem[0] += 1
        return nc.alloc_semaphore(name)

    def sb(name, shape, dt=F32):
        return nc.alloc_sbuf_tensor(name, shape, dt)

    bank = [nc.alloc_psum_tensor(f"bank{n}", [128, 512], F32) for n in range(8)]

    slots_in = nc.dram_tensor("slots_in", [ALL_SLOTS, D], F32, kind="Internal").ap()
    slots_out = nc.dram_tensor("slots_out", [ALL_SLOTS, D], F32, kind="Internal").ap()

    h = sb("h", [HT, NT, D])
    con = sb("con", [128, C_ALL])
    ident = con[:, C_IDENT:C_IDENT + 128]
    ones = con[:, C_ONES:C_ONES + 128]
    mask_bf = sb("mask_bf", [HT, 2, 492], BF16)
    ident_bf = sb("ident_bf", [HT, HT], BF16)
    logits = sb("logits", [HT, NT, E])

    arena = sb("arena", [128, ARENA])
    cur = [0]

    def cut(parts, *shape):
        n = 1
        for extent in shape:
            n *= extent
        ap = arena[0:parts, cur[0]:cur[0] + n]
        cur[0] += n
        assert cur[0] <= ARENA, cur[0]
        if len(shape) == 1:
            return ap
        names = "abcd"[:len(shape)]
        return ap.rearrange(f"p ({' '.join(names)}) -> p {' '.join(names)}", **dict(zip(names, shape)))

    wq_s, wk_s, wv_s, wo_s = (cut(DH, 2, D) for _ in range(4))
    ffn_in_s = cut(DH, 2, F)
    ffn_out_s = cut(128, FM, D)
    ffn_bias_s = cut(128, FM)
    w_attn_s = cut(DH, 2, 3 * D)
    w_proj_s = cut(128, 3, D)
    w_router_s = cut(DH, 2, E)
    qk_bias_s = cut(DH, 2, 2)
    v_bias_s = cut(HT, D)
    proj_bias_s = cut(HT, 2, D)
    anchor_w_s = cut(DH, 2, 6)
    anchors_s = cut(DH, 2, 6)
    lam_s = cut(DH, 2)
    anchor_p = cut(DH, 2, 6)
    anchor_h = cut(DH, 2)
    k_shift = cut(DH, 2)
    tok_bias_s = cut(PB, D)
    tok_b_s = cut(PB, D)
    zeros_src = cut(128, D)
    shared = cur[0]
    x1 = cut(HT, 2, D)
    x2 = cut(HT, 2, D)
    x3 = cut(HT, 2, D)
    x4 = cut(HT, 2, D)
    x1T, x2T, x3T, x4T = (cut(DH, 2, T) for _ in range(4))
    q0p = cut(DH, 3, 2, T)
    k0 = cut(DH, 2, T)
    v0 = cut(HT, 2, D)
    q1b = cut(DH, 2, T)
    q1p = cut(DH, 6, 2, T)
    k1 = cut(DH, 2, T)
    v1 = cut(HT, 2, H1, 32)
    p0 = cut(HT, 2, H0, T)
    p0T = cut(HT, 2, H0, T)
    p1a = cut(HT, H1, HT)
    p1b = cut(HT, H1, T)
    p1aT = cut(HT, H1, T)
    p1bT = cut(HT, H1, HT)
    sum0 = cut(HT, 2, H0)
    sum1 = cut(HT, 2, H1)
    inv0 = cut(HT, 2, H0)
    inv1 = cut(HT, 2, H1)
    att0 = cut(DH, 2 * T)
    att1 = cut(128, 3 * T)
    hid = cut(128, FM, T)
    nmax0 = cut(HT, 2, H0)
    nmax1 = cut(HT, 2, H1)
    stats = [cut(HT, 2, 6) for _ in range(4)]
    mv = [cut(HT, 2, 2) for _ in range(4)]
    var_eps = [cut(HT, 2) for _ in range(4)]
    rstd = [cut(HT, 2) for _ in range(4)]
    cur[0] = shared
    patches = cut(128, PK, B * NPATCH)
    tok_w_s = cut(128, PK, D)
    emb = cut(PB, NPT, D)
    cur[0] = 0
    wi_s = [cut(DH, 2, F) for _ in range(E)]
    wo_moe_s = [cut(128, FM, D) for _ in range(E)]
    xin = [cut(CT, 2, D) for _ in range(2)]
    xinT = [cut(DH, 2, SLOTS) for _ in range(2)]
    hidT = [cut(128, FM, SLOTS) for _ in range(2)]
    y = [cut(CT, 2, D) for _ in range(2)]
    xg = cut(HT, GT, D)
    yg = cut(HT, TOPK * GT, D)
    out_g = cut(HT, GT, D)
    g_stats = cut(HT, GT, 6)
    g_mv = cut(HT, GT, 2)
    g_var = cut(HT, GT)
    g_rstd = cut(HT, GT)
    gate_g = cut(HT, TOPK * GT)
    r_p = cut(HT, NT, E)
    r_a = cut(HT, NT, E)
    r_sel = cut(HT, G * E * TOPK * GT)
    r_scan, r_before = (yg.rearrange("p n d -> p (n d)")[:, 1024 * n:1024 * (n + 1)] for n in range(2))
    r_m = cut(HT, NT)
    r_s = cut(HT, NT)
    r_inv = cut(HT, NT)
    r_e = cut(HT, G, TOPK, GT)
    r_pos = cut(HT, G, TOPK, GT)
    r_ok = cut(HT, G, TOPK, GT)
    r_slot = cut(HT, G, TOPK, GT)
    r_tmp = cut(HT, G, TOPK, GT)
    gate = cut(HT, G, TOPK, GT)
    to_slot = sb("to_slot", [HT, G, TOPK * GT], U32)
    from_slot = sb("from_slot", [HT, G, TOPK * GT], U32)
    to_slot_g = sb("to_slot_g", [HT, TOPK * GT], U32)
    from_slot_g = sb("from_slot_g", [HT, TOPK * GT], U32)

    def bank_of(name):
        return bank[USES[PLACE[name]][2]]

    def p0T_unit(u):
        kt, m = u // 2, u % 2
        return p0T[:, kt, 3 * m:3 * m + 3, :].rearrange("p a b -> p (a b)")

    def p1T_unit(u):
        if u < 4:
            return p1aT[:, 3 * u:3 * u + 3, :].rearrange("p a b -> p (a b)")
        return p1bT[:, 6 * (u - 4):6 * (u - 4) + 6, :].rearrange("p a b -> p (a b)")

    def p0_rows(u):
        t, m = u // 2, u % 2
        return p0[:, t, 3 * m:3 * m + 3, :], inv0[:, t, 3 * m:3 * m + 3].unsqueeze(2).to_broadcast([HT, 3, T])

    def p1_rows(u):
        if u < 2:
            heads = slice(6 * u, 6 * u + 6)
            return p1a[:, heads, :], inv1[:, 0, heads].unsqueeze(2).to_broadcast([HT, 6, HT])
        heads = slice(3 * (u - 2), 3 * (u - 2) + 3)
        return p1b[:, heads, :], inv1[:, 1, heads].unsqueeze(2).to_broadcast([HT, 3, T])

    full = {n: sem(f"{n}_in_psum") for n, _, _ in USES}
    taken = {n: sem(f"{n}_taken") for n, _, _ in USES}
    weights_in = sem("weights_in")
    consts_in = sem("consts_in")
    patches_in = sem("patches_in")
    text_in = sem("text_in")
    zeros_out = sem("zeros_out")
    pool_setup = sem("pool_setup")
    vec_setup = sem("vec_setup")
    tok_full = sem("tok_full")
    tok_taken = sem("tok_taken")
    emb_in = sem("emb_in")
    h_emb = sem("h_emb")
    stats_made = [sem(f"stats{n + 1}_made") for n in range(4)]
    first_stats_made = sem("first_stats_made")
    mv_made = [sem(f"mv{n + 1}_made") for n in range(4)]
    var_made = [sem(f"var{n + 1}_made") for n in range(4)]
    rstd_made = [sem(f"rstd{n + 1}_made") for n in range(4)]
    x_made = [sem(f"x{n + 1}_made") for n in range(4)]
    nmax0_made = sem("nmax0_made")
    nmax1_made = sem("nmax1_made")
    inv0_made = sem("inv0_made")
    inv1_made = sem("inv1_made")
    p0_by_dve = sem("p0_by_dve")
    p0_by_pool = sem("p0_by_pool")
    p1_by_dve = sem("p1_by_dve")
    p1_by_pool = sem("p1_by_pool")
    proj_bias_added = sem("proj_bias_added")
    q1p_act = sem("q1p_act")
    q1p_dve = sem("q1p_dve")

    XN = [x1, x2, x3, x4]

    def wait(eng, s, value):
        if isinstance(value, int) and value <= 0:
            return
        eng.wait_ge(s, value)

    def wait_apart(eng, s, value):
        if not isinstance(value, int):
            value = eng.snap(value)
            eng.wait_ge(consts_in, 16)
        wait(eng, s, value)

    def need(eng, name, i):
        wait(eng, full[name], rounds(name, i))

    def have(eng, name, i):
        wait(eng, taken[name], rounds(name, i))

    def tile2(i):
        return h[:, bass.ds(2 * i, 2), :] if not isinstance(i, int) else h[:, 2 * i:2 * i + 2, :]

    def tile1(i, t):
        return h[:, bass.ds(2 * i + t, 1), :] if not isinstance(i, int) else h[:, 2 * i + t:2 * i + t + 1, :]

    def batch_loop(eng, body):
        body(0, True, False, True)
        body(1, True, True, True)
        with eng.Fori(2, B - 1) as i:
            body(i, True, True, True)
        body(B - 1, True, True, False)
        body(B, False, True, False)

    with nc.Block() as blk:
        @blk.sync
        def _(sp):
            def load(dst, src, s=weights_in):
                sp.dma_start(dst, src).then_inc(s, 16)

            sp.dma_start(con[:, :], consts).then_inc(consts_in, 16)
            sp.dma_start(tok_w_s, tok_w.rearrange("(k p) e -> p k e", p=128)).then_inc(patches_in, 16)
            sp.dma_start(tok_bias_s, tok_bias).then_inc(patches_in, 16)
            sp.dma_start(tok_b_s, tok_b).then_inc(patches_in, 16)
            pv = patchesT.rearrange("(k p) n -> p k n", p=128)
            for k in range(PK):
                sp.dma_start(patches[:, k, :], pv[:, k, :]).then_inc(patches_in, 16)
            for dst, src in ((wq_s, wq), (wk_s, wk), (wv_s, wv), (wo_s, wo), (ffn_in_s, ffn_in)):
                load(dst, src.rearrange("(c p) n -> p c n", p=DH))
            load(anchor_w_s, anchor_w)
            load(anchors_s, anchors)
            load(lam_s, lam)
            load(ffn_out_s, ffn_out.rearrange("(m p) n -> p m n", p=128))
            load(ffn_bias_s, ffn_bias)
            load(w_attn_s, w_attn.rearrange("(c p) n -> p c n", p=DH))
            load(w_router_s, w_router.rearrange("(c p) n -> p c n", p=DH))
            load(qk_bias_s, qk_bias)
            load(v_bias_s, v_bias)
            load(proj_bias_s, proj_bias)
            sp.wait_ge(pool_setup, 1)
            for r in range(4):
                load(w_proj_s[32 * r:32 * r + HD1, :, :],
                     w_proj.rearrange("(m r d) n -> r d m n", m=3, r=4)[r])
            hv = h[:, :, :].rearrange("p (b t) d -> p b t d", t=2)
            nfirst = HT - NPATCH
            for b0 in range(0, B, 8):
                sp.dma_start(hv[NPATCH:HT, b0:b0 + 8, 0, :],
                             txt[b0:b0 + 8, 0:nfirst, :].rearrange("b p d -> p b d")).then_inc(text_in, 16)
                sp.dma_start(hv[:, b0:b0 + 8, 1, :],
                             txt[b0:b0 + 8, nfirst:NTXT, :].rearrange("b p d -> p b d")).then_inc(text_in, 16)
            sp.wait_ge(tok_taken, NPT)
            for b3 in range(3):
                n = len(range(b3, B, 3))
                sp.dma_start(hv[0:NPATCH, b3:B:3, 0, :],
                             emb[NPATCH * b3:NPATCH * b3 + NPATCH, 0:n, :]).then_inc(h_emb, 16)
            sp.wait_ge(pool_setup, 2)
            sp.dma_start(slots_in.rearrange("(p a) d -> p a d", p=128),
                         zeros_src.unsqueeze(1).to_broadcast([128, ALL_SLOTS // 128, D])).then_inc(zeros_out, 16)
            sp.dma_start(slots_out.rearrange("(p a) d -> p a d", p=128),
                         zeros_src.unsqueeze(1).to_broadcast([128, ALL_SLOTS // 128, D])).then_inc(zeros_out, 16)
            sp.wait_ge(zeros_out, 32)

        @blk.gpsimd
        def _(pool):
            nc.gpsimd.memset(w_proj_s, 0.0).then_inc(pool_setup, 1)
            nc.gpsimd.memset(zeros_src, 0.0).then_inc(pool_setup, 1)
            pool.wait_ge(h_emb, 48)
            nc.gpsimd.memset(v1, 0.0).then_inc(pool_setup, 1)
            pool.wait_ge(consts_in, 16)
            pool.wait_ge(weights_in, 16 * N_WEIGHTS)

            def inv_std(n, count):
                pool.wait_ge(var_made[n], count)
                nc.gpsimd.tensor_tensor(rstd[n], var_eps[n], con[0:HT, C_HALF:C_HALF + 2],
                                        ALU.pow).then_inc(rstd_made[n], 1)

            inv_std(0, 1)

            def over_sum0(u, i):
                pool.wait_ge(inv0_made, 4 * i + u + 1)
                rows, inv = p0_rows(u)
                nc.gpsimd.tensor_tensor(rows, rows, inv, ALU.mult).then_inc(p0_by_pool, 1)

            def over_sum1(u, i):
                pool.wait_ge(inv1_made, 6 * i - 6 + u + 1)
                rows, inv = p1_rows(u)
                nc.gpsimd.tensor_tensor(rows, rows, inv, ALU.mult).then_inc(p1_by_pool, 1)

            def body(i, l0, l1, ahead):
                if l1:
                    inv_std(2, i)
                    pool.wait_ge(x_made[2], i)
                    hb = tile2(i - 1)
                    nc.gpsimd.tensor_tensor(hb, hb, proj_bias_s, ALU.add).then_inc(proj_bias_added, 1)
                if l0:
                    over_sum0(1, i)
                    over_sum0(3, i)
                if ahead:
                    inv_std(0, i + 2)
                if l1:
                    over_sum1(1, i)
                    over_sum1(3, i)
                if l0:
                    inv_std(1, i + 1)
                if l1:
                    inv_std(3, i)

            batch_loop(pool, body)

        @blk.tensor
        def _(pe):
            mm, tr = nc.tensor.matmul, nc.tensor.transpose
            pe.wait_ge(consts_in, 16)
            pe.wait_ge(patches_in, 16 * (3 + PK))
            for n in range(NPT):
                m = min(PB, B * NPATCH - n * PB)
                if n >= 4:
                    pe.wait_ge(tok_taken, n - 3)
                for k in range(PK):
                    op = mm(bank[n % 4][0:m, 0:D], patches[:, k, n * PB:n * PB + m], tok_w_s[:, k, :],
                            start=(k == 0), stop=(k == PK - 1))
                op.then_inc(tok_full, 1)
            pe.wait_ge(weights_in, 16 * N_WEIGHTS)
            pe.wait_ge(vec_setup, 2)

            def body(i, l0, l1, ahead):
                def free(name):
                    at = PLACE[name]
                    for back, n in [(0, n) for n in range(at - 1, -1, -1)] + [(1, n) for n in range(len(USES) - 1, at - 1, -1)]:
                        other, layer, where = USES[n]
                        if where != USES[at][2]:
                            continue
                        if not back and not (l1 if layer else ahead if other in AHEAD else l0):
                            continue
                        if isinstance(i, int) and back:
                            last = i - 1
                            ran = last >= (1 if layer else -1 if other in AHEAD else 0)
                            if not ran or (not layer and last > B - 1) or (other in AHEAD and last > B - 2):
                                continue
                        wait(pe, taken[other], rounds(other, i, back))
                        return bank[where]
                    return bank[USES[at][2]]

                def turn(name, x, b=None):
                    b = b or free(name)
                    for c in range(2):
                        for t in range(2):
                            op = tr(b[0:DH, c * T + t * HT:c * T + (t + 1) * HT], x[:, t, c * DH:(c + 1) * DH],
                                    ident[0:HT, 0:HT])
                    op.then_inc(full[name], 1)

                def stationary(name, w, col, xT, b=None):
                    b = b or free(name)
                    for m in range(2):
                        for c in range(2):
                            op = mm(b[0:DH, m * T:(m + 1) * T], w[:, c, col + m * DH:col + (m + 1) * DH],
                                    xT[:, c, :], start=(c == 0), stop=(c == 1))
                    op.then_inc(full[name], 1)

                def moving(name, w, col, xT, n=D, b=None):
                    b = b or free(name)
                    for t in range(2):
                        for c in range(2):
                            op = mm(b[0:HT, t * n:(t + 1) * n], xT[:, c, t * HT:(t + 1) * HT],
                                    w[:, c, col:col + n], start=(c == 0), stop=(c == 1))
                    op.then_inc(full[name], 1)

                def scores0(u):
                    t, m = u // 2, u % 2
                    b = free(f"scores0_{u}")
                    for j in range(3):
                        op = mm(b[0:HT, j * T:(j + 1) * T], q0p[:, j, m, t * HT:(t + 1) * HT], k0[:, m, :],
                                start=True, stop=True)
                    op.then_inc(full[f"scores0_{u}"], 1)

                def scores1(u):
                    b = free(f"scores1_{u}")
                    mm(b[0:HT, 0:492], ident_bf[:, :], mask_bf[:, 0 if u < 2 else 1, :], start=True, stop=False)
                    if u < 2:
                        for j in range(6):
                            op = mm(b[0:HT, j * HT:(j + 1) * HT], q1p[:, j, u, 0:HT], k1[:, u, 0:HT],
                                    start=False, stop=(j == 5))
                    else:
                        for j in range(3):
                            hd = 3 * (u - 2) + j
                            op = mm(b[0:HT, j * T:(j + 1) * T], q1p[:, hd % 6, hd // 6, HT:T], k1[:, hd // 6, :],
                                    start=False, stop=(j == 2))
                    op.then_inc(full[f"scores1_{u}"], 1)

                def probs0(u):
                    kt, m = u // 2, u % 2
                    b = free(f"probs0T_{u}")
                    pe.wait_ge(p0_by_pool if m else p0_by_dve, 2 * i + 2)
                    for j in range(3):
                        for t in range(2):
                            op = tr(b[0:HT, j * T + t * HT:j * T + (t + 1) * HT],
                                    p0[:, t, 3 * m + j, kt * HT:(kt + 1) * HT], ident[0:HT, 0:HT])
                    op.then_inc(full[f"probs0T_{u}"], 1)

                def probs1(u):
                    b = free(f"probs1T_{u}")
                    for s, k in {0: ((p1_by_dve, 2),), 1: ((p1_by_dve, 1), (p1_by_pool, 2)),
                                 2: ((p1_by_pool, 1), (p1_by_dve, 3)), 3: ((p1_by_pool, 1), (p1_by_dve, 4)),
                                 4: ((p1_by_dve, 2), (p1_by_pool, 2)), 5: ((p1_by_dve, 4),)}[u]:
                        pe.wait_ge(s, (4 if s is p1_by_dve else 2) * (i - 1) + k)
                    if u < 4:
                        for j in range(3):
                            hd = 3 * u + j
                            tr(b[0:HT, j * T:j * T + HT], p1a[:, hd, :], ident[0:HT, 0:HT])
                            op = tr(b[0:HT, j * T + HT:(j + 1) * T], p1b[:, hd, 0:HT], ident[0:HT, 0:HT])
                    else:
                        for j in range(6):
                            hd = 6 * (u - 4) + j
                            op = tr(b[0:HT, j * HT:(j + 1) * HT], p1b[:, hd, HT:T], ident[0:HT, 0:HT])
                    op.then_inc(full[f"probs1T_{u}"], 1)

                def weigh0():
                    b = free("att0")
                    for m in range(2):
                        for kt in range(2):
                            have(pe, f"probs0T_{2 * kt + m}", i)
                            for r in range(3):
                                hd = 3 * m + r
                                op = mm(b[32 * r:32 * r + 32, m * T:(m + 1) * T], v0[:, kt, 32 * hd:32 * hd + 32],
                                        p0T[:, kt, hd, :], start=(kt == 0), stop=(kt == 1))
                    op.then_inc(full["att0"], 1)

                def weigh1(*blocks):
                    b = free("att1") if blocks[0] == 0 else bank_of("att1")
                    for m in blocks:
                        have(pe, f"probs1T_{(4 * m + 3) // 3}", i)
                        for r in range(4):
                            hd = 4 * m + r
                            mm(b[32 * r:32 * r + 32, m * T:(m + 1) * T], v1[:, 0, hd, :], p1aT[:, hd, :],
                               start=True, stop=False)
                        have(pe, f"probs1T_{4 + (4 * m + 3) // 6}", i)
                        for r in range(4):
                            hd = 4 * m + r
                            op = mm(b[32 * r:32 * r + 32, m * T + HT:(m + 1) * T], v1[:, 1, hd, :], p1bT[:, hd, :],
                                    start=False, stop=True)
                    if blocks[-1] == 2:
                        op.then_inc(full["att1"], 1)

                if isinstance(i, int) and i == 0:
                    pe.wait_ge(x_made[0], 1)
                    turn("x1T", x1, bank_of("x1T"))
                    pe.wait_ge(taken["x1T"], 1)
                    stationary("q0", wq_s, 0, x1T, bank_of("q0"))
                    pe.wait_ge(taken["q0"], 1)
                    stationary("k0", wk_s, 0, x1T, bank_of("k0"))
                    pe.wait_ge(taken["k0"], 1)
                    moving("v0", wv_s, 0, x1T, b=bank_of("v0"))
                if l0:
                    wait(pe, taken["q0"], i + 1)
                    wait(pe, taken["k0"], i + 1)
                    for u in range(3):
                        scores0(u)
                if l1:
                    pe.wait_ge(x_made[2], i)
                    turn("x3T", x3)
                if l0:
                    scores0(3)
                if l1:
                    have(pe, "x3T", i)
                    stationary("q1", w_attn_s, 0, x3T)
                    stationary("k1", w_attn_s, D, x3T)
                    moving("v1", w_attn_s, 2 * D, x3T)
                    pe.wait_ge(q1p_act, i)
                    pe.wait_ge(q1p_dve, i)
                    have(pe, "k1", i)
                if l1:
                    scores1(0)
                    scores1(1)
                for n in range(4):
                    if l0:
                        probs0(P0_ORDER[n])
                    if l1:
                        scores1(2 + n)
                if l0:
                    wait(pe, taken["v0"], i + 1)
                    weigh0()
                if l1:
                    probs1(P1_ORDER[0])
                    probs1(P1_ORDER[1])
                if ahead:
                    pe.wait_ge(x_made[0], i + 2)
                    turn("x1T", x1)
                if l0:
                    have(pe, "att0", i)
                    b = free("proj0")
                    for t in range(2):
                        for m in range(2):
                            op = mm(b[0:HT, t * D:(t + 1) * D], att0[:, m * T + t * HT:m * T + (t + 1) * HT],
                                    wo_s[:, m, :], start=(m == 0), stop=(m == 1))
                    op.then_inc(full["proj0"], 1)
                if l1:
                    probs1(P1_ORDER[2])
                    probs1(P1_ORDER[3])
                    have(pe, "v1", i)
                    weigh1(0)
                    probs1(P1_ORDER[4])
                    probs1(P1_ORDER[5])
                if ahead:
                    have(pe, "x1T", i)
                    moving("v0", wv_s, 0, x1T)
                if l1:
                    weigh1(1, 2)
                if l0:
                    pe.wait_ge(x_made[1], i + 1)
                    turn("x2T", x2)
                if ahead:
                    stationary("q0", wq_s, 0, x1T)
                if l1:
                    have(pe, "att1", i)
                    b = free("proj1")
                    for t in range(2):
                        for m in range(3):
                            op = mm(b[0:HT, t * D:(t + 1) * D], att1[:, m * T + t * HT:m * T + (t + 1) * HT],
                                    w_proj_s[:, m, :], start=(m == 0), stop=(m == 2))
                    op.then_inc(full["proj1"], 1)
                if l0:
                    have(pe, "x2T", i)
                    for half, name in enumerate(("hid_a", "hid_b")):
                        b = free(name)
                        for j in range(3):
                            m = 3 * half + j
                            for c in range(2):
                                op = mm(b[:, j * T:(j + 1) * T], ffn_in_s[:, c, m * 128:(m + 1) * 128],
                                        x2T[:, c, :], start=(c == 0), stop=(c == 1))
                        op.then_inc(full[name], 1)
                if l0:
                    b = free("ffn")
                    have(pe, "hid_a", i)
                for t in range(2):
                    if l1 and t == 1:
                        pe.wait_ge(x_made[3], i)
                        turn("x4T", x4)
                    if l0:
                        for m in range(FM):
                            if t == 0 and m == 3:
                                have(pe, "hid_b", i)
                            op = mm(b[0:HT, t * D:(t + 1) * D], hid[:, m, t * HT:(t + 1) * HT],
                                    ffn_out_s[:, m, :], start=(m == 0), stop=(m == FM - 1))
                if l0:
                    op.then_inc(full["ffn"], 1)
                if ahead:
                    stationary("k0", wk_s, 0, x1T)
                if l1:
                    have(pe, "x4T", i)
                    moving("logits", w_router_s, 0, x4T, n=E)

            batch_loop(pe, body)

        @blk.vector
        def _(dve):
            V = nc.vector
            dve.wait_ge(consts_in, 16)
            V.tensor_copy(ident_bf[:, :], ident[0:HT, 0:HT]).then_inc(vec_setup, 1)
            V.tensor_copy(mask_bf[:, :, :].rearrange("p a b -> p (a b)"),
                          con[0:HT, C_MASK_A:C_MASK_A + 984]).then_inc(vec_setup, 1)
            dve.wait_ge(patches_in, 16 * (3 + PK))
            V.tensor_tensor(tok_bias_s, tok_bias_s, tok_b_s, ALU.add).then_inc(vec_setup, 1)
            dve.wait_ge(vec_setup, 3)
            for n in range(NPT):
                m = min(PB, B * NPATCH - n * PB)
                dve.wait_ge(tok_full, n + 1)
                V.tensor_tensor(emb[0:m, n, :], bank[n % 4][0:m, 0:D], tok_bias_s[0:m, :],
                                ALU.add).then_inc(tok_taken, 1)
            dve.wait_ge(weights_in, 16 * N_WEIGHTS)
            V.tensor_tensor(anchor_p, anchor_w_s, anchors_s,
                            ALU.mult).then_inc(vec_setup, 1)
            dve.wait_ge(vec_setup, 4)
            V.tensor_reduce(anchor_h, anchor_p, AX.X, ALU.add).then_inc(vec_setup, 1)
            dve.wait_ge(vec_setup, 5)
            V.scalar_tensor_tensor(out=k_shift, in0=anchor_h, scalar=float(HD0) ** 0.5,
                                   in1=lam_s, op0=ALU.mult, op1=ALU.mult).then_inc(vec_setup, 1)
            dve.wait_ge(vec_setup, 6)
            dve.wait_ge(h_emb, 48)
            dve.wait_ge(text_in, 16 * 8)

            def norm_stats(n, b, made):
                for t in range(2):
                    op = V.bn_stats(stats[n][:, t, :], tile1(b, t).rearrange("p a d -> p (a d)"))
                op.then_inc(made, 1)

            def norm_var(n, made, made_count, count):
                wait_apart(dve, made, made_count)
                for t in range(2):
                    op = V.bn_aggr(mv[n][:, t, :], stats[n][:, t, :])
                op.then_inc(mv_made[n], 1)
                dve.wait_ge(mv_made[n], count)
                V.tensor_scalar(var_eps[n], mv[n][:, :, 1], EPS, None, ALU.add).then_inc(var_made[n], 1)

            def norm_apply(n, b, count):
                dve.wait_ge(rstd_made[n], count)
                for t in range(2):
                    op = V.tensor_scalar(XN[n][:, t, :], tile1(b, t).rearrange("p a d -> p (a d)"),
                                         mv[n][:, t, 0:1], rstd[n][:, t:t + 1], ALU.subtract, ALU.mult)
                op.then_inc(x_made[n], 1)

            def top0(u, i):
                t, m = u // 2, u % 2
                need(dve, f"scores0_{u}", i)
                V.tensor_reduce(nmax0[:, t, 3 * m:3 * m + 3],
                                bank_of(f"scores0_{u}")[0:HT, 0:3 * T].rearrange("p (h k) -> p h k", h=3),
                                AX.X, ALU.max, negate=True).then_inc(nmax0_made, 1)

            def top1(u, i):
                need(dve, f"scores1_{u}", i)
                o, n = (nmax1[:, 0, 6 * u:6 * u + 6], 6) if u < 2 else (nmax1[:, 1, 3 * u - 6:3 * u - 3], 3)
                V.tensor_reduce(o, bank_of(f"scores1_{u}")[0:HT, 0:492].rearrange("p (h k) -> p h k", h=n),
                                AX.X, ALU.max, negate=True).then_inc(nmax1_made, 1)

            def invert0(u, i):
                t, m = u // 2, u % 2
                have(dve, f"scores0_{u}", i)
                V.reciprocal(inv0[:, t, 3 * m:3 * m + 3], sum0[:, t, 3 * m:3 * m + 3]).then_inc(inv0_made, 1)

            def invert1(u, i):
                have(dve, f"scores1_{u}", i)
                t, heads = (0, slice(6 * u, 6 * u + 6)) if u < 2 else (1, slice(3 * u - 6, 3 * u - 3))
                V.reciprocal(inv1[:, t, heads], sum1[:, t, heads]).then_inc(inv1_made, 1)

            def over_sum0(u, i):
                dve.wait_ge(inv0_made, 4 * i + u + 1)
                rows, inv = p0_rows(u)
                V.tensor_tensor(rows, rows, inv, ALU.mult).then_inc(p0_by_dve, 1)

            def over_sum1(u, i):
                dve.wait_ge(inv1_made, 6 * i - 6 + u + 1)
                rows, inv = p1_rows(u)
                V.tensor_tensor(rows, rows, inv, ALU.mult).then_inc(p1_by_dve, 1)

            def take_probs0(u, i):
                need(dve, f"probs0T_{u}", i)
                V.tensor_copy(p0T_unit(u), bank_of(f"probs0T_{u}")[0:HT, 0:492]).then_inc(taken[f"probs0T_{u}"], 1)

            def take_probs1(u, i):
                need(dve, f"probs1T_{u}", i)
                V.tensor_copy(p1T_unit(u), bank_of(f"probs1T_{u}")[0:HT, 0:492]).then_inc(taken[f"probs1T_{u}"], 1)

            norm_stats(0, 0, first_stats_made)
            norm_var(0, first_stats_made, 1, 1)
            norm_apply(0, 0, 1)

            def take_k0(i):
                need(dve, "k0", i)
                V.tensor_tensor(k0, bank_of("k0")[0:DH, 0:2 * T].rearrange("p (m t) -> p m t", m=2),
                                k_shift.unsqueeze(2).to_broadcast([DH, 2, T]),
                                ALU.add).then_inc(taken["k0"], 1)

            take_k0(-1)

            def body(i, l0, l1, ahead):
                if l1:
                    norm_stats(2, i - 1, stats_made[2])
                    norm_var(2, stats_made[2], i, i)
                if l0:
                    top0(0, i)
                if l1:
                    norm_apply(2, i - 1, i)
                if l0:
                    for u in (1, 2):
                        top0(u, i)
                if l1:
                    need(dve, "x3T", i)
                    V.tensor_copy(x3T.rearrange("p c t -> p (c t)"), bank_of("x3T")[0:DH, 0:2 * T]).then_inc(taken["x3T"], 1)
                if l0:
                    top0(3, i)
                    invert0(0, i)
                    invert0(1, i)
                    over_sum0(0, i)
                if l1:
                    need(dve, "q1", i)
                    V.tensor_tensor(q1b, bank_of("q1")[0:DH, 0:2 * T].rearrange("p (m t) -> p m t", m=2),
                                    qk_bias_s[:, 0, :].unsqueeze(2).to_broadcast([DH, 2, T]),
                                    ALU.add).then_inc(taken["q1"], 1)
                    have(dve, "q1", i)
                    for j in range(2, 6):
                        op = V.tensor_scalar(q1p[:, j, :, :], q1b, con[0:DH, C_QM1 + j:C_QM1 + j + 1], None, ALU.mult)
                    op.then_inc(q1p_dve, 1)
                if l0:
                    invert0(2, i)
                    invert0(3, i)
                if l1:
                    need(dve, "k1", i)
                    V.tensor_tensor(k1, bank_of("k1")[0:DH, 0:2 * T].rearrange("p (m t) -> p m t", m=2),
                                    qk_bias_s[:, 1, :].unsqueeze(2).to_broadcast([DH, 2, T]),
                                    ALU.add).then_inc(taken["k1"], 1)
                if l0:
                    over_sum0(2, i)
                if l1:
                    need(dve, "v1", i)
                    for t in range(2):
                        op = V.tensor_tensor(v1[:, t, :, 0:HD1],
                                             bank_of("v1")[0:HT, t * D:(t + 1) * D].rearrange("p (h d) -> p h d", h=H1),
                                             v_bias_s.rearrange("p (h d) -> p h d", h=H1), ALU.add)
                    op.then_inc(taken["v1"], 1)
                if ahead:
                    norm_stats(0, i + 1, stats_made[0])
                if l1:
                    top1(0, i)
                    top1(1, i)
                if l0:
                    take_probs0(P0_ORDER[0], i)
                if ahead:
                    norm_var(0, stats_made[0], i + 1, i + 2)
                if l1:
                    invert1(0, i)
                    top1(2, i)
                    over_sum1(0, i)
                if l0:
                    take_probs0(P0_ORDER[1], i)
                if l1:
                    invert1(1, i)
                    top1(3, i)
                if ahead:
                    norm_apply(0, i + 1, i + 2)
                if l1:
                    invert1(2, i)
                    over_sum1(2, i)
                    top1(4, i)
                    invert1(3, i)
                if l0:
                    take_probs0(P0_ORDER[3], i)
                if l1:
                    top1(5, i)
                if l1:
                    invert1(4, i)
                if l0:
                    need(dve, "att0", i)
                    V.tensor_copy(att0, bank_of("att0")[0:DH, 0:2 * T]).then_inc(taken["att0"], 1)
                if l1:
                    over_sum1(4, i)
                    invert1(5, i)
                    over_sum1(5, i)
                    take_probs1(P1_ORDER[1], i)
                if l0:
                    need(dve, "proj0", i)
                    V.tensor_tensor(tile2(i), bank_of("proj0")[0:HT, 0:2 * D].rearrange("p (t d) -> p t d", t=2),
                                    tile2(i), ALU.add).then_inc(taken["proj0"], 1)
                if l1:
                    take_probs1(P1_ORDER[3], i)
                if l0:
                    wait_apart(dve, taken["proj0"], rounds("proj0", i))
                    norm_stats(1, i, stats_made[1])
                    norm_var(1, stats_made[1], i + 1, i + 1)
                if l1:
                    take_probs1(P1_ORDER[5], i)
                if l0:
                    norm_apply(1, i, i + 1)
                if l1:
                    need(dve, "proj1", i)
                    wait(dve, proj_bias_added, i)
                    V.tensor_tensor(tile2(i - 1), bank_of("proj1")[0:HT, 0:2 * D].rearrange("p (t d) -> p t d", t=2),
                                    tile2(i - 1), ALU.add).then_inc(taken["proj1"], 1)
                    wait_apart(dve, taken["proj1"], rounds("proj1", i))
                    norm_stats(3, i - 1, stats_made[3])
                    norm_var(3, stats_made[3], i, i)
                    norm_apply(3, i - 1, i)
                if l0:
                    need(dve, "ffn", i)
                    V.tensor_tensor(tile2(i), bank_of("ffn")[0:HT, 0:2 * D].rearrange("p (t d) -> p t d", t=2),
                                    tile2(i), ALU.add).then_inc(taken["ffn"], 1)
                if ahead:
                    take_k0(i)
                if l1:
                    need(dve, "logits", i)
                    lt = logits[:, bass.ds(2 * i - 2, 2), :] if not isinstance(i, int) else logits[:, 2 * i - 2:2 * i, :]
                    V.tensor_scalar(lt, bank_of("logits")[0:HT, 0:2 * E].rearrange("p (t e) -> p t e", t=2),
                                    1.0, None, ALU.mult).then_inc(taken["logits"], 1)
                if l0:
                    have(dve, "ffn", i)

            batch_loop(dve, body)

        @blk.scalar
        def _(act):
            A = nc.scalar.activation
            act.wait_ge(consts_in, 16)
            act.wait_ge(weights_in, 16 * N_WEIGHTS)
            act.wait_ge(h_emb, 48)

            def take(name, dst, parts, cols, i):
                need(act, name, i)
                A(dst, bank_of(name)[0:parts, 0:cols], ACT.Copy).then_inc(taken[name], 1)

            act.wait_ge(full["x1T"], 1)
            A(x1T.rearrange("p c t -> p (c t)"), bank_of("x1T")[0:DH, 0:2 * T], ACT.Copy).then_inc(taken["x1T"], 1)

            def take_q0(i):
                need(act, "q0", i)
                for j in range(3):
                    op = A(q0p[:, j, :, :].rearrange("p m t -> p (m t)"), bank_of("q0")[0:DH, 0:2 * T], ACT.Copy,
                           scale=con[0:DH, C_QM0 + j:C_QM0 + j + 1])
                op.then_inc(taken["q0"], 1)

            take_q0(-1)
            act.wait_ge(full["v0"], 1)
            A(v0.rearrange("p t d -> p (t d)"), bank_of("v0")[0:HT, 0:2 * D], ACT.Copy).then_inc(taken["v0"], 1)

            def exps0(u, i):
                t, m = u // 2, u % 2
                act.wait_ge(nmax0_made, 4 * i + u + 1)
                for j in range(3):
                    hd = 3 * m + j
                    op = A(p0[:, t, hd, :], bank_of(f"scores0_{u}")[0:HT, j * T:(j + 1) * T], ACT.Exp,
                           bias=nmax0[:, t, hd:hd + 1], accum_out=sum0[:, t, hd:hd + 1])
                op.then_inc(taken[f"scores0_{u}"], 1)

            def exps1(u, i):
                act.wait_ge(nmax1_made, 6 * i - 6 + u + 1)
                t, dst, n, w, first = (0, p1a, 6, HT, 6 * u) if u < 2 else (1, p1b, 3, T, 3 * u - 6)
                for j in range(n):
                    hd = first + j
                    op = A(dst[:, hd, :], bank_of(f"scores1_{u}")[0:HT, j * w:(j + 1) * w], ACT.Exp,
                           bias=nmax1[:, t, hd:hd + 1], accum_out=sum1[:, t, hd:hd + 1])
                op.then_inc(taken[f"scores1_{u}"], 1)

            def body(i, l0, l1, ahead):
                if l0:
                    for u in range(4):
                        exps0(u, i)
                if l1:
                    have(act, "q1", i)
                    for j in range(2):
                        op = A(q1p[:, j, :, :], q1b, ACT.Copy, scale=con[0:DH, C_QM1 + j:C_QM1 + j + 1])
                    op.then_inc(q1p_act, 1)
                    exps1(0, i)
                    exps1(1, i)
                for n in range(4):
                    if l0 and n == 2:
                        u = P0_ORDER[n]
                        take(f"probs0T_{u}", p0T_unit(u), HT, 492, i)
                    if l1:
                        exps1(2 + n, i)
                if l1:
                    take(f"probs1T_{P1_ORDER[0]}", p1T_unit(P1_ORDER[0]), HT, 492, i)
                if ahead:
                    take("x1T", x1T.rearrange("p c t -> p (c t)"), DH, 2 * T, i)
                if l1:
                    for u in P1_ORDER[2::2]:
                        take(f"probs1T_{u}", p1T_unit(u), HT, 492, i)
                if ahead:
                    take("v0", v0.rearrange("p t d -> p (t d)"), HT, 2 * D, i)
                if l1:
                    take("att1", att1, 128, 3 * T, i)
                if l0:
                    take("x2T", x2T.rearrange("p c t -> p (c t)"), DH, 2 * T, i)
                if ahead:
                    take_q0(i)
                if l0:
                    for half, name in enumerate(("hid_a", "hid_b")):
                        need(act, name, i)
                        for j in range(3):
                            m = 3 * half + j
                            op = A(hid[:, m, :], bank_of(name)[:, j * T:(j + 1) * T], ACT.Gelu,
                                   bias=ffn_bias_s[:, m:m + 1])
                        op.then_inc(taken[name], 1)
                if l1:
                    take("x4T", x4T.rearrange("p c t -> p (c t)"), DH, 2 * T, i)

            batch_loop(act, body)

    moe_in = [sem(f"expert{e}_weights_in") for e in range(E)]
    routed = sem("routed")
    exps_made = sem("exps_made")
    places_made = sem("places_made")
    xg_stats = sem("xg_stats")
    xg_first_stats = sem("xg_first_stats")
    xg_mv = sem("xg_mv")
    xg_var = sem("xg_var")
    xg_rstd = sem("xg_rstd")
    xg_made = sem("xg_made")
    to_copied = sem("scatter_indices_copied")
    from_copied = sem("gather_indices_copied")
    scattered = sem("scattered")
    gathered = sem("gathered")
    gates_copied = sem("gates_copied")
    first_added = sem("first_added")
    combined = sem("combined")
    out_stored = sem("out_stored")
    xin_in = [sem(f"xin{n}_in") for n in range(2)]
    turned = sem("turned")
    turn_taken = sem("turn_taken")
    hid_full = sem("hid_full")
    hid_taken = sem("hid_taken")
    y_full = sem("y_full")
    y_taken = sem("y_taken")
    y_out = [sem(f"y{n}_out") for n in range(2)]
    turn_bank, hid_banks, y_banks, place_banks = bank[0], bank[1:4], bank[4:6], bank[6:8]

    def group_loop(eng, body):
        body(0, True, False)
        with eng.Fori(1, G - 1) as g:
            body(g, True, True)
        body(G - 1, False, True)

    with nc.Block() as blk:
        @blk.sync
        def _(sp):
            for e in range(E):
                sp.dma_start(wi_s[e], wi[e].rearrange("(c p) f -> p c f", p=DH)).then_inc(moe_in[e], 16)
                sp.dma_start(wo_moe_s[e], wo_moe[e].rearrange("(m p) d -> p m d", p=128)).then_inc(moe_in[e], 16)

            def load(g, e):
                n = 8 * g + e
                wait(sp, turned, n - 1)
                rows = slots_in.rearrange("(n t p) d -> n p t d", t=2, p=CT)
                src = rows[n] if isinstance(n, int) else rows[bass.ds(n, 1)].rearrange("a p t d -> (a p) t d")
                sp.dma_start(xin[e % 2], src).then_inc(xin_in[e % 2], 16)

            def body(g, ahead, behind):
                sp.wait_ge(scattered, 256 * g + 256)
                for e in range(E):
                    load(g, e)

            group_loop(sp, body)

        @blk.gpsimd
        def _(pool):
            P = nc.gpsimd

            def scatter(g):
                wait(pool, xg_var, g + 1)
                P.tensor_tensor(g_rstd, g_var, con[0:HT, C_HALF:C_HALF + GT], ALU.pow).then_inc(xg_rstd, 1)
                wait(pool, scattered, 256 * g)
                src = to_slot[:, g, :] if isinstance(g, int) else to_slot[:, bass.ds(g, 1), :].rearrange("p a n -> p (a n)")
                P.tensor_copy(to_slot_g[:, :], src).then_inc(to_copied, 1)
                wait_apart(pool, to_copied, g + 1)
                wait(pool, xg_made, g + 1)
                for k in range(TOPK):
                    for t in range(GT):
                        n = k * GT + t
                        P.indirect_dma_start(
                            out=slots_in, out_offset=bass.IndirectOffsetOnAxis(ap=to_slot_g[:, n:n + 1], axis=0),
                            in_=xg[:, t, :], in_offset=None, bounds_check=ALL_SLOTS - 1,
                            oob_is_err=False).then_inc(scattered, 16)

            def gather(g):
                for n in range(2):
                    wait(pool, y_out[n], 64 * g + 64)
                wait(pool, combined, g)
                src = from_slot[:, g, :] if isinstance(g, int) else from_slot[:, bass.ds(g, 1), :].rearrange("p a n -> p (a n)")
                P.tensor_copy(from_slot_g[:, :], src).then_inc(from_copied, 1)
                wait_apart(pool, from_copied, g + 1)
                for n in range(TOPK * GT):
                    P.indirect_dma_start(
                        out=yg[:, n, :], out_offset=None, in_=slots_out,
                        in_offset=bass.IndirectOffsetOnAxis(ap=from_slot_g[:, n:n + 1], axis=0),
                        bounds_check=ALL_SLOTS - 1, oob_is_err=False).then_inc(gathered, 16)
                wait(pool, combined, g + 1)
                dst = out_rows[g] if isinstance(g, int) else out_rows[bass.ds(g, 1)].rearrange("a p t d -> (a p) t d")
                P.dma_start(dst, out_g).then_inc(out_stored, 16)

            out_rows = out.rearrange("b (t p) d -> (b t) p d", p=HT).rearrange("(g t) p d -> g p t d", t=GT)
            pool.wait_ge(routed, ROUTED)
            scatter(0)

            def body(g, ahead, behind):
                if ahead:
                    scatter(g + 1)
                if behind:
                    gather(g - 1)

            group_loop(pool, body)
            gather(G - 1)
            pool.wait_ge(out_stored, 16 * G)

        @blk.tensor
        def _(pe):
            mm, tr = nc.tensor.matmul, nc.tensor.transpose
            pe.wait_ge(routed, R_BEFORE)
            for n in range(2):
                mm(place_banks[n][0:HT, :], con[0:HT, C_TRI:C_TRI + HT], r_sel[:, 512 * n:512 * (n + 1)],
                   start=True, stop=False)
                mm(place_banks[n][0:HT, :], ones[0:HT, 0:HT], r_before[:, 512 * n:512 * (n + 1)],
                   start=False, stop=True).then_inc(places_made, 1)

            def turn(g, e):
                n = 8 * g + e
                pe.wait_ge(xin_in[e % 2], 64 * g + 16 * (e // 2) + 16)
                wait(pe, turn_taken, n)
                for c in range(2):
                    for t in range(2):
                        op = tr(turn_bank[0:DH, c * SLOTS + t * CT:c * SLOTS + (t + 1) * CT],
                                xin[e % 2][:, t, c * DH:(c + 1) * DH], ident[0:CT, 0:CT])
                op.then_inc(turned, 1)

            def up(g, e):
                n = 8 * g + e
                pe.wait_ge(moe_in[e], 32)
                wait(pe, turn_taken, n + 1)
                for j in range(3):
                    wait(pe, hid_taken, 3 * n - 2 + j)
                    for k in range(2):
                        m = 2 * j + k
                        for c in range(2):
                            op = mm(hid_banks[j][:, k * SLOTS:(k + 1) * SLOTS], wi_s[e][:, c, m * 128:(m + 1) * 128],
                                    xinT[e % 2][:, c, :], start=(c == 0), stop=(c == 1))
                    op.then_inc(hid_full, 1)

            def down(g, e):
                n = 8 * g + e
                wait(pe, hid_taken, 3 * n + 3)
                wait(pe, y_taken, n - 1)
                for t in range(2):
                    for m in range(FM):
                        op = mm(y_banks[e % 2][0:CT, t * D:(t + 1) * D], hidT[e % 2][:, m, t * CT:(t + 1) * CT],
                                wo_moe_s[e][:, m, :], start=(m == 0), stop=(m == FM - 1))
                op.then_inc(y_full, 1)

            def after(g, e, k):
                return (g, e + k) if e + k < E else (g + 1, e + k - E)

            turn(0, 0)
            turn(0, 1)
            up(0, 0)

            def body(g, ahead, behind):
                for e in range(E):
                    if ahead or e + 2 < E:
                        turn(*after(g, e, 2))
                    if ahead or e + 1 < E:
                        up(*after(g, e, 1))
                    down(g, e)

            group_loop(pe, body)

        @blk.vector
        def _(dve):
            V = nc.vector
            step = [0]

            def link(op):
                step[0] += 1
                op.then_inc(routed, 1)
                dve.wait_ge(routed, step[0])

            def by_expert(ap):
                return ap.unsqueeze(2).to_broadcast([HT, NT, E])

            rev = con[0:HT, C_REV:C_REV + E].unsqueeze(1).to_broadcast([HT, NT, E])
            flat = "p a b c -> p (a b c)"
            sel = r_sel.rearrange("p (g e k t) -> p g e k t", g=G, e=E, k=TOPK)
            link(V.tensor_reduce(r_m, logits[:, :, :], AX.X, ALU.max))
            link(V.tensor_tensor(r_a, logits[:, :, :], by_expert(r_m), ALU.subtract))
            dve.wait_ge(exps_made, 1)
            link(V.tensor_reduce(r_s, r_p, AX.X, ALU.add))
            link(V.reciprocal(r_inv, r_s))
            link(V.tensor_tensor(r_p, r_p, by_expert(r_inv), ALU.mult))
            for k in range(TOPK):
                link(V.tensor_reduce(r_m, r_p, AX.X, ALU.max))
                link(V.tensor_copy(gate[:, :, k, :], r_m.rearrange("p (g t) -> p g t", g=G)))
                link(V.tensor_tensor(r_a, r_p, by_expert(r_m), ALU.is_equal))
                link(V.tensor_tensor(r_a, r_a, rev, ALU.mult))
                link(V.tensor_reduce(r_s, r_a, AX.X, ALU.max))
                link(V.tensor_copy(r_e[:, :, k, :], r_s.rearrange("p (g t) -> p g t", g=G)))
                link(V.tensor_tensor(r_a, rev, by_expert(r_s), ALU.is_equal))
                link(V.tensor_copy(sel[:, :, :, k, :], r_a.rearrange("p (g t) e -> p g e t", g=G)))
                if k == 0:
                    link(V.scalar_tensor_tensor(out=r_p, in0=r_a, scalar=-2.0, in1=r_p, op0=ALU.mult, op1=ALU.add))
            link(V.tensor_tensor_scan(r_scan, con[0:HT, C_RESET:C_RESET + 1024], r_sel, 0.0, ALU.mult, ALU.add))
            link(V.tensor_tensor(r_before, r_scan, r_sel, ALU.subtract))
            assert step[0] == R_BEFORE, step[0]
            for n in range(2):
                dve.wait_ge(places_made, n + 1)
                link(V.tensor_tensor(r_scan[:, 512 * n:512 * (n + 1)], place_banks[n][0:HT, :],
                                     r_sel[:, 512 * n:512 * (n + 1)], ALU.mult))
            link(V.tensor_reduce(r_pos.rearrange("p g k t -> p g (k t)"),
                                 r_scan.rearrange("p (g e n) -> p g n e", g=G, e=E), AX.X, ALU.add))
            pos, ok, slot, tmp, best, gates = (x.rearrange(flat) for x in (r_pos, r_ok, r_slot, r_tmp, r_e, gate))
            base = con[0:HT, C_BASE:C_BASE + 128]
            link(V.tensor_scalar(ok, pos, float(CAP), None, ALU.is_lt))
            link(V.tensor_scalar(slot, best, -float(SLOTS), float(E * SLOTS), ALU.mult, ALU.add))
            link(V.tensor_tensor(slot, slot, pos, ALU.add))
            link(V.tensor_scalar(tmp, ok, -BIG, BIG, ALU.mult, ALU.add))
            link(V.tensor_tensor(tmp, tmp, slot, ALU.add))
            link(V.tensor_tensor(tmp, tmp, base, ALU.add))
            link(V.tensor_copy(to_slot[:, :, :].rearrange("p g n -> p (g n)"), tmp))
            link(V.scalar_tensor_tensor(out=slot, in0=slot, scalar=float(SLOTS - 1), in1=ok,
                                        op0=ALU.subtract, op1=ALU.mult))
            link(V.scalar_tensor_tensor(out=slot, in0=slot, scalar=float(SLOTS - 1), in1=base,
                                        op0=ALU.add, op1=ALU.add))
            link(V.tensor_copy(from_slot[:, :, :].rearrange("p g n -> p (g n)"), slot))
            link(V.tensor_tensor(gates, gates, ok, ALU.mult))
            assert step[0] == ROUTED, step[0]

            def at(ap, g):
                return ap[:, g:g + 1] if isinstance(g, int) else ap[:, bass.ds(g, 1)]

            def group_norm(g, made, count):
                for t in range(GT):
                    op = V.bn_stats(g_stats[:, t, :], at(h, 8 * g + t).rearrange("p a d -> p (a d)"))
                op.then_inc(made, 1)
                wait_apart(dve, made, count)
                for t in range(GT):
                    op = V.bn_aggr(g_mv[:, t, :], g_stats[:, t, :])
                op.then_inc(xg_mv, 1)
                dve.wait_ge(xg_mv, g + 1)
                V.tensor_scalar(g_var, g_mv[:, :, 1], EPS, None, ALU.add).then_inc(xg_var, 1)
                wait(dve, scattered, 256 * g)
                dve.wait_ge(xg_rstd, g + 1)
                for t in range(GT):
                    op = V.tensor_scalar(xg[:, t, :], at(h, 8 * g + t).rearrange("p a d -> p (a d)"),
                                         g_mv[:, t, 0:1], g_rstd[:, t:t + 1], ALU.subtract, ALU.mult)
                op.then_inc(xg_made, 1)

            def combine(g):
                wait(dve, combined, g)
                V.tensor_copy(gate_g.rearrange("p (k t) -> p k t", k=TOPK),
                              gate[:, g, :, :] if isinstance(g, int) else
                              gate[:, bass.ds(g, 1), :, :].rearrange("p a k t -> p (a k) t")).then_inc(gates_copied, 1)
                dve.wait_ge(gates_copied, g + 1)
                dve.wait_ge(gathered, 256 * g + 256)
                wait(dve, out_stored, 16 * g)
                for t in range(GT):
                    op = V.scalar_tensor_tensor(out=out_g[:, t, :], in0=yg[:, t, :], scalar=gate_g[:, t:t + 1],
                                                in1=at(h, 8 * g + t).rearrange("p a d -> p (a d)"),
                                                op0=ALU.mult, op1=ALU.add)
                op.then_inc(first_added, 1)
                dve.wait_ge(first_added, g + 1)
                for t in range(GT):
                    op = V.scalar_tensor_tensor(out=out_g[:, t, :], in0=yg[:, GT + t, :],
                                                scalar=gate_g[:, GT + t:GT + t + 1], in1=out_g[:, t, :],
                                                op0=ALU.mult, op1=ALU.add)
                op.then_inc(combined, 1)

            group_norm(0, xg_first_stats, 1)

            def body(g, ahead, behind):
                if ahead:
                    group_norm(g + 1, xg_stats, g + 1)
                if behind:
                    combine(g - 1)

            group_loop(dve, body)
            combine(G - 1)

        @blk.scalar
        def _(act):
            A = nc.scalar.activation
            act.wait_ge(routed, 2)
            A(r_p, r_a, ACT.Exp).then_inc(exps_made, 1)

            def turn(g, e):
                n = 8 * g + e
                act.wait_ge(turned, n + 1)
                A(xinT[e % 2].rearrange("p c s -> p (c s)"), turn_bank[0:DH, 0:2 * SLOTS], ACT.Copy).then_inc(turn_taken, 1)

            def up(g, e):
                n = 8 * g + e
                for j in range(3):
                    act.wait_ge(hid_full, 3 * n + j + 1)
                    A(hidT[e % 2][:, 2 * j:2 * j + 2, :].rearrange("p m s -> p (m s)"),
                      hid_banks[j][:, 0:2 * SLOTS], ACT.Relu).then_inc(hid_taken, 1)

            rows = slots_out.rearrange("(n t p) d -> n p t d", t=2, p=CT)

            def down(g, e):
                n = 8 * g + e
                act.wait_ge(y_full, n + 1)
                wait(act, y_out[e % 2], 64 * g + 16 * (e // 2))
                A(y[e % 2].rearrange("p t d -> p (t d)"), y_banks[e % 2][0:CT, 0:2 * D], ACT.Copy).then_inc(y_taken, 1)
                act.wait_ge(y_taken, n + 1)
                dst = rows[n] if isinstance(n, int) else rows[bass.ds(n, 1)].rearrange("a p t d -> (a p) t d")
                act.dma_start(dst, y[e % 2]).then_inc(y_out[e % 2], 16)

            def after(g, e, k):
                return (g, e + k) if e + k < E else (g + 1, e + k - E)

            turn(0, 0)
            turn(0, 1)
            up(0, 0)

            def body(g, ahead, behind):
                for e in range(E):
                    if ahead or e + 2 < E:
                        turn(*after(g, e, 2))
                    if ahead or e + 1 < E:
                        up(*after(g, e, 1))
                    down(g, e)

            group_loop(act, body)
            for n in range(2):
                act.wait_ge(y_out[n], 64 * G)


R_BEFORE = 24
ROUTED = 38


def constants():
    import numpy as np
    c = np.zeros((128, C_ALL), np.float32)
    p = np.arange(128)
    c[:, C_IDENT:C_IDENT + 128] = np.eye(128)
    c[:, C_ONES:C_ONES + 128] = 1.0
    for j in range(3):
        c[(p // HD0) == j, C_QM0 + j] = HD0 ** -0.5
    for j in range(6):
        c[(p // HD1) == j, C_QM1 + j] = HD1 ** -0.5
    causal = np.where(np.arange(HT)[None, :] <= p[:, None], 0.0, MASKED)
    c[:, C_MASK_A:C_MASK_A + 492] = np.tile(causal, (1, 6))
    c[:, C_MASK_B:C_MASK_B + 492] = np.tile(np.concatenate([np.zeros((128, HT)), causal], 1), (1, 3))
    c[:, C_TRI:C_TRI + HT] = p[:, None] < np.arange(HT)[None, :]
    c[:, C_REV:C_REV + E] = E - np.arange(E)
    c[:, C_RESET:C_RESET + 1024] = np.arange(1024) % (TOPK * GT) != 0
    c[:, C_BASE:C_BASE + 128] = np.repeat(np.arange(G) * GROUP_SLOTS, TOPK * GT)
    c[:, C_HALF:C_HALF + 8] = -0.5
    return c


def kernel(x, txt, L0_tok_W, L0_tok_b, L0_tok_pos_embed, L0_attn_Wq, L0_attn_Wk, L0_attn_Wv, L0_attn_Wo,
           L0_attn_anchor_w, L0_attn_anchors, L0_attn_lam, L0_ffn_in_weight, L0_ffn_in_bias, L0_ffn_out_weight,
           L1_attn_w_attn, L1_attn_b_attn, L1_attn_w_proj, L1_attn_b_proj, L1_ffn_w_router, L1_ffn_wi, L1_ffn_wo):
    import numpy as np
    import concourse.bacc as bacc
    from concourse.bass_utils import run_bass_kernel_spmd

    def rows(a, n):
        return np.broadcast_to(np.asarray(a), (n,) + np.shape(a))

    def halves(a):
        a = np.asarray(a)
        return np.moveaxis(a.reshape((2, DH) + a.shape[1:]), 0, 1)

    patches = np.asarray(x).reshape(B, 3, 6, 16, 6, 16).transpose(1, 3, 5, 0, 2, 4).reshape(PATCH_DIM, B * NPATCH)
    b_attn = np.asarray(L1_attn_b_attn)
    arrays = {
        "patchesT": patches,
        "txt": txt,
        "tok_w": np.asarray(L0_tok_W).T,
        "tok_bias": np.tile(np.asarray(L0_tok_pos_embed)[0], (3, 1)),
        "tok_b": rows(L0_tok_b, PB),
        "wq": np.asarray(L0_attn_Wq).T,
        "wk": np.asarray(L0_attn_Wk).T,
        "wv": np.asarray(L0_attn_Wv).T,
        "wo": np.asarray(L0_attn_Wo).T,
        "anchor_w": halves(np.asarray(L0_attn_anchor_w).reshape(D, 6)),
        "anchors": halves(np.repeat(np.asarray(L0_attn_anchors), HD0, 0)),
        "lam": halves(np.repeat(np.asarray(L0_attn_lam), HD0)),
        "ffn_in": np.asarray(L0_ffn_in_weight).T,
        "ffn_bias": np.asarray(L0_ffn_in_bias).reshape(FM, 128).T,
        "ffn_out": L0_ffn_out_weight,
        "w_attn": L1_attn_w_attn,
        "qk_bias": np.moveaxis(b_attn[:2 * D].reshape(2, 2, DH), 2, 0),
        "v_bias": rows(b_attn[2 * D:], HT),
        "w_proj": L1_attn_w_proj,
        "proj_bias": rows(rows(L1_attn_b_proj, 2), HT),
        "w_router": L1_ffn_w_router,
        "wi": L1_ffn_wi,
        "wo_moe": L1_ffn_wo,
        "consts": constants(),
    }
    nc = bacc.Bacc("TRN2", target_bir_lowering=False, num_devices=1)
    given, args = {}, {}
    for name, a in arrays.items():
        a = np.ascontiguousarray(a)
        given[f"in_{name}"] = a
        args[name] = nc.dram_tensor(f"in_{name}", a.shape, mybir.dt.from_np(a.dtype), kind="ExternalInput").ap()
    out = nc.dram_tensor("out", (B, T, D), F32, kind="ExternalOutput").ap()
    program(nc, out=out, **args)
    r = run_bass_kernel_spmd(nc, [given], core_ids=[0])
    return r.results[0]["out"]
```

```python
import concourse.bass as bass
from concourse import mybir

F32 = mybir.dt.float32
BF16 = mybir.dt.bfloat16
U32 = mybir.dt.uint32
ALU = mybir.AluOpType
ACT = mybir.ActivationFunctionType
AX = mybir.AxisListType

B, NPATCH, NTXT, D = 32, 36, 128, 192
T = NPATCH + NTXT
HT = T // 2
NT = 2 * B
DH = D // 2
PATCH_DIM = 768
PK = PATCH_DIM // 128
F = 768
FM = F // 128
H0, HD0 = 6, 32
H1, HD1 = 12, 16
EPS = 1e-5
E, TOPK = 8, 2
G = 8
GT = NT // G
S = GT * HT
CAP = int(TOPK * 1.25 * S / E)
CT = (CAP + 1) // 2
SLOTS = 2 * CT
GROUP_SLOTS = E * SLOTS
ALL_SLOTS = G * GROUP_SLOTS
BIG = 1.0e6
MASKED = -1.0e30
ARENA = 36900
PB = 3 * NPATCH
N_WEIGHTS = 16
NPT = -(-B // 3)
CONSTS = 48
PART = (0, 4, 8, NPT)

C_IDENT = 0
C_ONES = 128
C_QM0 = 256
C_QM1 = C_QM0 + 3
C_MASK_A = 272
C_MASK_B = C_MASK_A + 492
C_TRI = C_MASK_B + 492
C_REV = C_TRI + HT
C_RESET = C_REV + E
C_BASE = C_RESET + 1024
C_HALF = C_BASE + 128
C_ALL = C_HALF + 8

USES = []
S1_ORDER = (0, 2, 1, 3, 4, 5)
P0_ORDER = (0, 2, 1, 3)
P1_ORDER = (0, 1, 4, 5, 2, 3)


def _uses():
    ring = {"scores": [0, 1, 2], "probs": [3, 4]}
    seen = dict.fromkeys(ring, 0)

    def use(layer, kind, *names):
        for name in names:
            banks = ring[kind]
            USES.append((name, layer, banks[seen[kind] % len(banks)]))
            seen[kind] += 1

    use(0, "scores", *[f"scores0_{u}" for u in range(4)])
    use(1, "scores", *[f"scores1_{u}" for u in S1_ORDER])
    use(0, "probs", *[f"probs0T_{u}" for u in P0_ORDER])
    use(1, "probs", *[f"probs1T_{u}" for u in P1_ORDER])
    USES.extend([("x3T", 1, 5), ("q1", 1, 6), ("k1", 1, 7), ("v1", 1, 5), ("att0", 0, 6), ("x1T", 0, 7),
                 ("proj0", 0, 5), ("att1", 1, 6), ("k0", 0, 7), ("x2T", 0, 5), ("q0", 0, 7), ("proj1", 1, 5),
                 ("hid_a", 0, 6), ("hid_b", 0, 7), ("ffn", 0, 5), ("x4T", 1, 6), ("v0", 0, 7), ("logits", 1, 6)])


_uses()
PLACE = {name: n for n, (name, _, _) in enumerate(USES)}
AHEAD = ("x1T", "v0", "q0", "k0")


def rounds(name, i, back=0):
    layer = USES[PLACE[name]][1]
    if name in AHEAD:
        return i + 2 - back
    return i + (1 - layer) - back


def program(nc, patchesT, txt, tok_w, tok_bias, tok_b, wq, wk, wv, wo, anchor_w, anchors, lam,
            ffn_in, ffn_bias, ffn_out, w_attn, qk_bias, v_bias, w_proj, proj_bias,
            w_router, wi, wo_moe, consts, out):
    nsem = [0]

    def sem(name):
        nsem[0] += 1
        return nc.alloc_semaphore(name)

    def sb(name, shape, dt=F32):
        return nc.alloc_sbuf_tensor(name, shape, dt)

    bank = [nc.alloc_psum_tensor(f"bank{n}", [128, 512], F32) for n in range(8)]

    slots_in = nc.dram_tensor("slots_in", [ALL_SLOTS, D], F32, kind="Internal").ap()
    slots_out = nc.dram_tensor("slots_out", [ALL_SLOTS, D], F32, kind="Internal").ap()

    h = sb("h", [HT, NT, D])
    con = sb("con", [128, C_ALL])
    h_by_batch = h[:, :, :].rearrange("p (b t) d -> p b t d", t=2)
    ident = con[:, C_IDENT:C_IDENT + 128]
    ones = con[:, C_ONES:C_ONES + 128]
    mask_bf = sb("mask_bf", [HT, 2, 492], BF16)
    ident_bf = sb("ident_bf", [HT, HT], BF16)
    logits = sb("logits", [HT, NT, E])

    arena = sb("arena", [128, ARENA])
    cur = [0]

    def cut(parts, *shape):
        n = 1
        for extent in shape:
            n *= extent
        ap = arena[0:parts, cur[0]:cur[0] + n]
        cur[0] += n
        assert cur[0] <= ARENA, cur[0]
        if len(shape) == 1:
            return ap
        names = "abcd"[:len(shape)]
        return ap.rearrange(f"p ({' '.join(names)}) -> p {' '.join(names)}", **dict(zip(names, shape)))

    wq_s, wk_s, wv_s, wo_s = (cut(DH, 2, D) for _ in range(4))
    ffn_in_s = cut(DH, 2, F)
    ffn_out_s = cut(128, FM, D)
    layer0_end = cur[0]
    ffn_bias_s = cut(128, FM)
    w_attn_s = cut(DH, 2, 3 * D)
    w_proj_s = cut(DH, 2, D)
    w_router_s = cut(DH, 2, E)
    qk_bias_s = cut(DH, 2, 2)
    v_bias_s = cut(HT, D)
    proj_bias_s = cut(HT, 2, D)
    anchor_w_s = cut(DH, 2, 6)
    anchors_s = cut(DH, 2, 6)
    lam_s = cut(DH, 2)
    anchor_p = cut(DH, 2, 6)
    anchor_h = cut(DH, 2)
    k_shift = cut(DH, 2)
    tok_bias_s = cut(PB, D)
    tok_b_s = cut(PB, D)
    zeros_src = cut(128, D)
    x1 = cut(HT, 2, D)
    x2 = cut(HT, 2, D)
    x3 = cut(HT, 2, D)
    x4 = cut(HT, 2, D)
    x1T, x2T, x3T, x4T = (cut(DH, 2, T) for _ in range(4))
    q0p = cut(DH, 3, 2, T)
    k0 = cut(DH, 2, T)
    v0 = cut(HT, 2, D)
    q1b = cut(DH, 2, T)
    q1p = cut(DH, 6, 2, T)
    k1 = cut(DH, 2, T)
    v1 = cut(HT, 2, H1, 32)
    p0 = cut(HT, 2, H0, T)
    p0T = cut(HT, 2, H0, T)
    p1a = cut(HT, H1, HT)
    p1b = cut(HT, H1, T)
    p1aT = cut(HT, H1, T)
    p1bT = cut(HT, H1, HT)
    sum0 = cut(HT, 2, H0)
    sum1 = cut(HT, 2, H1)
    inv0 = cut(HT, 2, H0)
    inv1 = cut(HT, 2, H1)
    att0 = cut(DH, 2 * T)
    att1 = cut(DH, 2 * T)
    nmax0 = cut(HT, 2, H0)
    nmax1 = cut(HT, 2, H1)
    stats = [cut(HT, 2, 6) for _ in range(4)]
    mv = [cut(HT, 2, 2) for _ in range(4)]
    var_eps = [cut(HT, 2) for _ in range(4)]
    rstd = [cut(HT, 2) for _ in range(4)]
    in_both = cur[0]
    hid = cut(128, FM, T)
    batch_end = cur[0]
    cur[0] = in_both
    patches = cut(128, PK, B * NPATCH)
    tok_w_s = cut(128, PK, D)
    emb = cut(PB, NPT, D)
    cur[0] = 0
    wi_s, wo_moe_s = [], []
    for _ in range(E):
        wi_s.append(cut(DH, 2, F))
        wo_moe_s.append(cut(128, FM, D))
    assert 2 * F + FM * D <= layer0_end
    xin = [cut(CT, 2, D) for _ in range(2)]
    xinT = [cut(DH, 2, SLOTS) for _ in range(2)]
    hidT = [cut(128, FM, SLOTS) for _ in range(2)]
    y = [cut(CT, 2, D) for _ in range(2)]
    out_g = cut(HT, GT, D)
    assert cur[0] >= batch_end
    xg = cut(HT, GT, D)
    yg = cut(HT, TOPK * GT, D)
    g_stats = cut(HT, GT, 6)
    g_mv = cut(HT, GT, 2)
    g_var = cut(HT, GT)
    g_rstd = cut(HT, GT)
    gate_g = cut(HT, TOPK * GT)
    r_p = cut(HT, NT, E)
    r_a = cut(HT, NT, E)
    r_sel = cut(HT, G * E * TOPK * GT)
    r_scan, r_before = (yg.rearrange("p n d -> p (n d)")[:, 1024 * n:1024 * (n + 1)] for n in range(2))
    r_m = cut(HT, NT)
    r_s = cut(HT, NT)
    r_inv = cut(HT, NT)
    r_e = cut(HT, G, TOPK, GT)
    r_pos = cut(HT, G, TOPK, GT)
    r_ok = cut(HT, G, TOPK, GT)
    r_slot = cut(HT, G, TOPK, GT)
    r_tmp = cut(HT, G, TOPK, GT)
    gate = cut(HT, G, TOPK, GT)
    to_slot = sb("to_slot", [HT, G, TOPK * GT], U32)
    from_slot = sb("from_slot", [HT, G, TOPK * GT], U32)
    to_slot_g = sb("to_slot_g", [HT, TOPK * GT], U32)
    from_slot_g = sb("from_slot_g", [HT, TOPK * GT], U32)

    def bank_of(name):
        return bank[USES[PLACE[name]][2]]

    def p0T_unit(u):
        kt, m = u // 2, u % 2
        return p0T[:, kt, 3 * m:3 * m + 3, :].rearrange("p a b -> p (a b)")

    def p1T_unit(u):
        if u < 4:
            return p1aT[:, 3 * u:3 * u + 3, :].rearrange("p a b -> p (a b)")
        return p1bT[:, 6 * (u - 4):6 * (u - 4) + 6, :].rearrange("p a b -> p (a b)")

    def p0_rows(u):
        t, m = u // 2, u % 2
        return p0[:, t, 3 * m:3 * m + 3, :], inv0[:, t, 3 * m:3 * m + 3].unsqueeze(2).to_broadcast([HT, 3, T])

    def p1_rows(u):
        if u < 2:
            heads = slice(6 * u, 6 * u + 6)
            return p1a[:, heads, :], inv1[:, 0, heads].unsqueeze(2).to_broadcast([HT, 6, HT])
        heads = slice(3 * (u - 2), 3 * (u - 2) + 3)
        return p1b[:, heads, :], inv1[:, 1, heads].unsqueeze(2).to_broadcast([HT, 3, T])

    full = {n: sem(f"{n}_in_psum") for n, _, _ in USES}
    taken = {n: sem(f"{n}_taken") for n, _, _ in USES}
    weights_in = sem("weights_in")
    consts_in = sem("consts_in")
    patches_in = [sem(f"patches{c}_in") for c in range(3)]
    text_in = sem("text_in")
    zeros_out = sem("zeros_out")
    pool_setup = sem("pool_setup")
    vec_setup = sem("vec_setup")
    act_setup = sem("act_setup")
    tok_full = sem("tok_full")
    tok_taken = sem("tok_taken")
    h_emb = [sem("h_first_emb"), sem("h_emb")]
    stats_made = [sem(f"stats{n + 1}_made") for n in range(4)]
    first_stats_made = sem("first_stats_made")
    mv_made = [sem(f"mv{n + 1}_made") for n in range(4)]
    var_made = [sem(f"var{n + 1}_made") for n in range(4)]
    rstd_made = [sem(f"rstd{n + 1}_made") for n in range(4)]
    x_made = [sem(f"x{n + 1}_made") for n in range(4)]
    nmax0_made = sem("nmax0_made")
    nmax1_made = sem("nmax1_made")
    inv0_made = sem("inv0_made")
    inv1_made = sem("inv1_made")
    p0_by_dve = sem("p0_by_dve")
    p0_by_pool = sem("p0_by_pool")
    p1_by_dve = sem("p1_by_dve")
    p1_by_pool = sem("p1_by_pool")
    proj_bias_added = sem("proj_bias_added")
    q1p_made = sem("q1p_made")

    moe_in = [sem("expert0_weights_in"), sem("expert1_weights_in")]
    for pair in range(1, E // 2):
        moe_in += [sem(f"experts{2 * pair}_{2 * pair + 1}_weights_in")] * 2
    routed = sem("routed")
    exps_made = sem("exps_made")
    places_made = sem("places_made")
    xg_stats = sem("xg_stats")
    xg_first_stats = sem("xg_first_stats")
    xg_mv = sem("xg_mv")
    xg_var = sem("xg_var")
    xg_rstd = sem("xg_rstd")
    xg_made = sem("xg_made")
    to_copied = sem("scatter_indices_copied")
    from_copied = sem("gather_indices_copied")
    scattered = sem("scattered")
    gathered = [sem(f"gathered_half{n}") for n in range(2)]
    gates_copied = sem("gates_copied")
    first_added = sem("first_added")
    combined = sem("combined")
    out_stored = sem("out_stored")
    xin_in = [sem(f"xin{n}_in") for n in range(2)]
    turned = sem("turned")
    turn_taken = sem("turn_taken")
    hid_full = sem("hid_full")
    hid_taken = sem("hid_taken")
    y_full = sem("y_full")
    y_taken = sem("y_taken")
    y_out = [sem(f"y{n}_out") for n in range(2)]
    turn_bank, hid_banks, y_banks, place_banks = bank[0], bank[1:4], bank[4:6], bank[6:8]

    XN = [x1, x2, x3, x4]

    def wait(eng, s, value):
        if isinstance(value, int) and value <= 0:
            return
        eng.wait_ge(s, value)

    def wait_apart(eng, s, value):
        if not isinstance(value, int):
            value = eng.snap(value)
            eng.wait_ge(consts_in, CONSTS)
        wait(eng, s, value)

    def need(eng, name, i):
        wait(eng, full[name], rounds(name, i))

    def have(eng, name, i):
        wait(eng, taken[name], rounds(name, i))

    def tile2(i):
        return h[:, bass.ds(2 * i, 2), :] if not isinstance(i, int) else h[:, 2 * i:2 * i + 2, :]

    def tile1(i, t):
        return h[:, bass.ds(2 * i + t, 1), :] if not isinstance(i, int) else h[:, 2 * i + t:2 * i + t + 1, :]

    def load_expert(sp, e):
        sp.dma_start(wi_s[e], wi[e].rearrange("(c p) f -> p c f", p=DH)).then_inc(moe_in[e], 16)
        sp.dma_start(wo_moe_s[e], wo_moe[e].rearrange("(m p) d -> p m d", p=128)).then_inc(moe_in[e], 16)

    def route_exps(act, g0, g1, before):
        act.wait_ge(routed, before + 2)
        nc.scalar.activation(r_p[:, GT * g0:GT * g1, :], r_a[:, GT * g0:GT * g1, :], ACT.Exp).then_inc(exps_made, 1)

    def route_places(pe, banks, g0, g1, before):
        pe.wait_ge(routed, before + R_BEFORE)
        for b, (c0, c1) in zip(banks, place_columns(g0, g1)):
            nc.tensor.matmul(b[0:HT, 0:c1 - c0], con[0:HT, C_TRI:C_TRI + HT], r_sel[:, c0:c1], start=True, stop=False)
            nc.tensor.matmul(b[0:HT, 0:c1 - c0], ones[0:HT, 0:HT], r_before[:, c0:c1],
                             start=False, stop=True).then_inc(places_made, 1)

    def place_columns(g0, g1):
        c0, c1 = GCOLS * g0, GCOLS * g1
        if c1 - c0 <= 512:
            return [(c0, c1)]
        return [(c0, (c0 + c1) // 2), ((c0 + c1) // 2, c1)]

    def route_views(g0, g1):
        tiles = slice(GT * g0, GT * g1)
        return (r_p[:, tiles, :], r_a[:, tiles, :], r_m[:, tiles], r_s[:, tiles],
                con[0:HT, C_REV:C_REV + E].unsqueeze(1).to_broadcast([HT, GT * (g1 - g0), E]))

    def by_expert(ap):
        return ap.unsqueeze(2).to_broadcast([HT, ap.shape[1], E])

    def linker(dve, before):
        step = [before]

        def link(op):
            step[0] += 1
            op.then_inc(routed, 1)
            dve.wait_ge(routed, step[0])

        return link, step

    def route_best(link, k, g0, g1):
        V, groups = nc.vector, slice(g0, g1)
        p, a, m, best, rev = route_views(g0, g1)
        sel = r_sel.rearrange("p (g e k t) -> p g e k t", g=G, e=E, k=TOPK)[:, groups]
        link(V.tensor_reduce(m, p, AX.X, ALU.max))
        link(V.tensor_copy(gate[:, groups, k, :], m.rearrange("p (g t) -> p g t", g=g1 - g0)))
        link(V.tensor_tensor(a, p, by_expert(m), ALU.is_equal))
        link(V.tensor_tensor(a, a, rev, ALU.mult))
        link(V.tensor_reduce(best, a, AX.X, ALU.max))
        link(V.tensor_copy(r_e[:, groups, k, :], best.rearrange("p (g t) -> p g t", g=g1 - g0)))
        link(V.tensor_tensor(a, rev, by_expert(best), ALU.is_equal))
        link(V.tensor_copy(sel[:, :, :, k, :], a.rearrange("p (g t) e -> p g e t", g=g1 - g0)))

    def route_start(dve, g0, g1, before, exps_before):
        V = nc.vector
        link, step = linker(dve, before)
        p, a, m, total, _ = route_views(g0, g1)
        inv = r_inv[:, GT * g0:GT * g1]
        link(V.tensor_reduce(m, logits[:, GT * g0:GT * g1, :], AX.X, ALU.max))
        link(V.tensor_tensor(a, logits[:, GT * g0:GT * g1, :], by_expert(m), ALU.subtract))
        dve.wait_ge(exps_made, exps_before + 1)
        link(V.tensor_reduce(total, p, AX.X, ALU.add))
        link(V.reciprocal(inv, total))
        link(V.tensor_tensor(p, p, by_expert(inv), ALU.mult))
        route_best(link, 0, g0, g1)
        assert step[0] == before + R_START, step[0]

    def route_second(dve, g0, g1, before):
        V = nc.vector
        link, step = linker(dve, before + R_START)
        p, a, _, _, _ = route_views(g0, g1)
        c0, c1 = GCOLS * g0, GCOLS * g1
        link(V.scalar_tensor_tensor(out=p, in0=a, scalar=-2.0, in1=p, op0=ALU.mult, op1=ALU.add))
        route_best(link, 1, g0, g1)
        link(V.tensor_tensor_scan(r_scan[:, c0:c1], con[0:HT, C_RESET:C_RESET + c1 - c0], r_sel[:, c0:c1], 0.0,
                                  ALU.mult, ALU.add))
        link(V.tensor_tensor(r_before[:, c0:c1], r_scan[:, c0:c1], r_sel[:, c0:c1], ALU.subtract))
        assert step[0] == before + R_BEFORE, step[0]

    def route_end(dve, banks, g0, g1, before, places_before):
        V = nc.vector
        link, step = linker(dve, before + R_BEFORE)
        groups, ng = slice(g0, g1), g1 - g0
        for n, (c0, c1) in enumerate(place_columns(g0, g1)):
            dve.wait_ge(places_made, places_before + n + 1)
            link(V.tensor_tensor(r_scan[:, c0:c1], banks[n][0:HT, 0:c1 - c0], r_sel[:, c0:c1], ALU.mult))
        link(V.tensor_reduce(r_pos[:, groups].rearrange("p g k t -> p g (k t)"),
                             r_scan[:, GCOLS * g0:GCOLS * g1].rearrange("p (g e n) -> p g n e", g=ng, e=E),
                             AX.X, ALU.add))
        pos, ok, slot, tmp, best, gates = (x[:, groups].rearrange("p a b c -> p (a b c)")
                                           for x in (r_pos, r_ok, r_slot, r_tmp, r_e, gate))
        base = con[0:HT, C_BASE + TOPK * GT * g0:C_BASE + TOPK * GT * g1]
        link(V.tensor_scalar(ok, pos, float(CAP), None, ALU.is_lt))
        link(V.tensor_scalar(slot, best, -float(SLOTS), float(E * SLOTS), ALU.mult, ALU.add))
        link(V.tensor_tensor(slot, slot, pos, ALU.add))
        link(V.tensor_scalar(tmp, ok, -BIG, BIG, ALU.mult, ALU.add))
        link(V.tensor_tensor(tmp, tmp, slot, ALU.add))
        link(V.tensor_tensor(tmp, tmp, base, ALU.add))
        link(V.tensor_copy(to_slot[:, groups, :].rearrange("p g n -> p (g n)"), tmp))
        link(V.scalar_tensor_tensor(out=slot, in0=slot, scalar=float(SLOTS - 1), in1=ok,
                                    op0=ALU.subtract, op1=ALU.mult))
        link(V.scalar_tensor_tensor(out=slot, in0=slot, scalar=float(SLOTS - 1), in1=base,
                                    op0=ALU.add, op1=ALU.add))
        link(V.tensor_copy(from_slot[:, groups, :].rearrange("p g n -> p (g n)"), slot))
        link(V.tensor_tensor(gates, gates, ok, ALU.mult))
        assert step[0] in (ROUTED_FIRST, ROUTED), step[0]

    def at(ap, g):
        return ap[:, g:g + 1] if isinstance(g, int) else ap[:, bass.ds(g, 1)]

    def group_stats(dve, g, made, count):
        for t in range(GT):
            op = nc.vector.bn_stats(g_stats[:, t, :], at(h, 8 * g + t).rearrange("p a d -> p (a d)"))
        op.then_inc(made, 1)
        wait_apart(dve, made, count)
        for t in range(GT):
            op = nc.vector.bn_aggr(g_mv[:, t, :], g_stats[:, t, :])
        op.then_inc(xg_mv, 1)
        dve.wait_ge(xg_mv, g + 1)
        nc.vector.tensor_scalar(g_var, g_mv[:, :, 1], EPS, None, ALU.add).then_inc(xg_var, 1)

    def group_apply(dve, g):
        wait(dve, scattered, 256 * g)
        dve.wait_ge(xg_rstd, g + 1)
        for t in range(GT):
            op = nc.vector.tensor_scalar(xg[:, t, :], at(h, 8 * g + t).rearrange("p a d -> p (a d)"),
                                         g_mv[:, t, 0:1], g_rstd[:, t:t + 1], ALU.subtract, ALU.mult)
        op.then_inc(xg_made, 1)

    def scatter_ready(pool, g):
        wait(pool, xg_var, g + 1)
        nc.gpsimd.tensor_tensor(g_rstd, g_var, con[0:HT, C_HALF:C_HALF + GT], ALU.pow).then_inc(xg_rstd, 1)
        if isinstance(g, int) and g == 0:
            pool.wait_ge(routed, ROUTED_FIRST)
        wait(pool, scattered, 256 * g)
        src = to_slot[:, g, :] if isinstance(g, int) else to_slot[:, bass.ds(g, 1), :].rearrange("p a n -> p (a n)")
        nc.gpsimd.tensor_copy(to_slot_g[:, :], src).then_inc(to_copied, 1)

    def scatter(pool, g):
        wait_apart(pool, to_copied, g + 1)
        wait(pool, xg_made, g + 1)
        for k in range(TOPK):
            for t in range(GT):
                n = k * GT + t
                nc.gpsimd.indirect_dma_start(
                    out=slots_in, out_offset=bass.IndirectOffsetOnAxis(ap=to_slot_g[:, n:n + 1], axis=0),
                    in_=xg[:, t, :], in_offset=None, bounds_check=ALL_SLOTS - 1,
                    oob_is_err=False).then_inc(scattered, 16)

    def batch_loop(eng, body, route_first=lambda: None):
        body(0, True, False, True)
        body(1, True, True, True)
        with eng.Fori(2, B - 1) as i:
            body(i, True, True, True)
        body(B - 1, True, True, False)
        route_first()
        body(B, False, True, False)

    def place_patches(eng, c):
        n0, n1 = PART[c], PART[c + 1]
        eng.wait_ge(tok_taken, n1)
        for b3 in range(3):
            n = len(range(3 * n0 + b3, min(3 * n1, B), 3))
            eng.dma_start(h_by_batch[0:NPATCH, 3 * n0 + b3:min(3 * n1, B):3, 0, :],
                          emb[NPATCH * b3:NPATCH * b3 + NPATCH, n0:n0 + n, :]).then_inc(h_emb[c > 0], 16)

    def embed_bank(n):
        return bank[3 + n % 4]

    with nc.Block() as blk:
        @blk.sync
        def _(sp):
            def load(dst, src, s=weights_in):
                sp.dma_start(dst, src).then_inc(s, 16)

            def load_text(b0, s):
                first = HT - NPATCH
                sp.dma_start(h_by_batch[NPATCH:HT, b0:b0 + 8, 0, :],
                             txt[b0:b0 + 8, 0:first, :].rearrange("b p d -> p b d")).then_inc(s, 16)
                sp.dma_start(h_by_batch[:, b0:b0 + 8, 1, :],
                             txt[b0:b0 + 8, first:NTXT, :].rearrange("b p d -> p b d")).then_inc(s, 16)

            pv = patchesT.rearrange("(k p) n -> p k n", p=128)
            sp.dma_start(tok_w_s, tok_w.rearrange("(k p) e -> p k e", p=128)).then_inc(patches_in[0], 16)
            for c in range(3):
                n0, n1 = PART[c] * PB, min(PART[c + 1] * PB, B * NPATCH)
                sp.dma_start(patches[:, :, n0:n1], pv[:, :, n0:n1]).then_inc(patches_in[c], 16)
                if c == 0:
                    sp.dma_start(tok_bias_s, tok_bias).then_inc(patches_in[0], 16)
                    sp.dma_start(tok_b_s, tok_b).then_inc(patches_in[0], 16)
                    load_text(0, consts_in)
                    sp.dma_start(con[:, :], consts).then_inc(consts_in, 16)
            for dst, src in ((wq_s, wq), (wk_s, wk), (wv_s, wv), (wo_s, wo), (ffn_in_s, ffn_in)):
                load(dst, src.rearrange("(c p) n -> p c n", p=DH))
            load(anchor_w_s, anchor_w)
            load(anchors_s, anchors)
            load(lam_s, lam)
            load(ffn_out_s, ffn_out.rearrange("(m p) n -> p m n", p=128))
            load(ffn_bias_s, ffn_bias)
            place_patches(sp, 0)
            load(w_attn_s, w_attn.rearrange("(c p) n -> p c n", p=DH))
            load(w_router_s, w_router.rearrange("(c p) n -> p c n", p=DH))
            load(qk_bias_s, qk_bias)
            load(v_bias_s, v_bias)
            load(proj_bias_s, proj_bias)
            load(w_proj_s, w_proj.rearrange("(c p) n -> p c n", p=DH))
            for b0 in range(8, B, 8):
                load_text(b0, text_in)
            place_patches(sp, 1)
            place_patches(sp, 2)
            sp.wait_ge(pool_setup, 1)
            sp.dma_start(slots_in.rearrange("(p a) d -> p a d", p=128),
                         zeros_src.unsqueeze(1).to_broadcast([128, ALL_SLOTS // 128, D])).then_inc(zeros_out, 16)
            sp.dma_start(slots_out.rearrange("(p a) d -> p a d", p=128),
                         zeros_src.unsqueeze(1).to_broadcast([128, ALL_SLOTS // 128, D])).then_inc(zeros_out, 16)
            sp.wait_ge(taken["ffn"], B)
            load_expert(sp, 0)

        @blk.gpsimd
        def _(pool):
            nc.gpsimd.memset(zeros_src, 0.0).then_inc(pool_setup, 1)
            nc.gpsimd.memset(v1, 0.0).then_inc(pool_setup, 1)
            pool.wait_ge(consts_in, CONSTS)

            def inv_std(n, count):
                pool.wait_ge(var_made[n], count)
                nc.gpsimd.tensor_tensor(rstd[n], var_eps[n], con[0:HT, C_HALF:C_HALF + 2],
                                        ALU.pow).then_inc(rstd_made[n], 1)

            inv_std(0, 1)
            pool.wait_ge(weights_in, 16 * N_WEIGHTS)

            def over_sum0(u, i):
                pool.wait_ge(inv0_made, 4 * i + u + 1)
                rows, inv = p0_rows(u)
                nc.gpsimd.tensor_tensor(rows, rows, inv, ALU.mult).then_inc(p0_by_pool, 1)

            def over_sum1(u, i):
                pool.wait_ge(inv1_made, 6 * i - 6 + S1_ORDER.index(u) + 1)
                rows, inv = p1_rows(u)
                nc.gpsimd.tensor_tensor(rows, rows, inv, ALU.mult).then_inc(p1_by_pool, 1)

            def body(i, l0, l1, ahead):
                if l1:
                    inv_std(2, i)
                if isinstance(i, int) and i == B:
                    scatter_ready(pool, 0)
                if l1:
                    pool.wait_ge(x_made[2], i)
                    hb = tile2(i - 1)
                    nc.gpsimd.tensor_tensor(hb, hb, proj_bias_s, ALU.add).then_inc(proj_bias_added, 1)
                if l0:
                    over_sum0(1, i)
                if l1:
                    have(pool, "q1", i)
                    scale = con[0:DH, C_QM1 + 2:C_QM1 + 3].unsqueeze(2).to_broadcast([DH, 2, T])
                    nc.gpsimd.tensor_tensor(q1p[:, 2, :, :], q1b, scale, ALU.mult).then_inc(q1p_made, 1)
                if l0:
                    over_sum0(3, i)
                if ahead:
                    inv_std(0, i + 2)
                if l1:
                    over_sum1(1, i)
                    over_sum1(3, i)
                if isinstance(i, int) and i == B:
                    pool.wait_ge(zeros_out, 32)
                    scatter(pool, 0)
                if l0:
                    inv_std(1, i + 1)
                if l1:
                    inv_std(3, i)

            batch_loop(pool, body)

        @blk.tensor
        def _(pe):
            mm, tr = nc.tensor.matmul, nc.tensor.transpose

            def embed(n):
                if n in PART:
                    pe.wait_ge(patches_in[PART.index(n)], 16 if n else 64)
                m = min(PB, B * NPATCH - n * PB)
                if n >= 4:
                    pe.wait_ge(tok_taken, n - 3)
                for k in range(PK):
                    op = mm(embed_bank(n)[0:m, 0:D], patches[:, k, n * PB:n * PB + m], tok_w_s[:, k, :],
                            start=(k == 0), stop=(k == PK - 1))
                op.then_inc(tok_full, 1)

            for n in range(PART[2] + 1):
                embed(n)
            pe.wait_ge(consts_in, CONSTS)
            pe.wait_ge(vec_setup, 2)
            pe.wait_ge(act_setup, 1)

            def body(i, l0, l1, ahead):
                def free(name):
                    place = PLACE[name]
                    earlier = [(0, n) for n in range(place - 1, -1, -1)]
                    earlier += [(1, n) for n in range(len(USES) - 1, place - 1, -1)]
                    for back, n in earlier:
                        other, layer, where = USES[n]
                        if where != USES[place][2]:
                            continue
                        if not back and not (l1 if layer else ahead if other in AHEAD else l0):
                            continue
                        if isinstance(i, int) and back:
                            last = i - 1
                            ran = last >= (1 if layer else -1 if other in AHEAD else 0)
                            if not ran or (not layer and last > B - 1) or (other in AHEAD and last > B - 2):
                                continue
                        wait(pe, taken[other], rounds(other, i, back))
                        return bank[where]
                    return bank[USES[place][2]]

                def turn(name, x, b=None):
                    b = b or free(name)
                    for c in range(2):
                        for t in range(2):
                            op = tr(b[0:DH, c * T + t * HT:c * T + (t + 1) * HT], x[:, t, c * DH:(c + 1) * DH],
                                    ident[0:HT, 0:HT])
                    op.then_inc(full[name], 1)

                def stationary(name, w, col, xT, b=None):
                    b = b or free(name)
                    for m in range(2):
                        for c in range(2):
                            op = mm(b[0:DH, m * T:(m + 1) * T], w[:, c, col + m * DH:col + (m + 1) * DH],
                                    xT[:, c, :], start=(c == 0), stop=(c == 1))
                    op.then_inc(full[name], 1)

                def moving(name, w, col, xT, n=D, b=None):
                    b = b or free(name)
                    for t in range(2):
                        for c in range(2):
                            op = mm(b[0:HT, t * n:(t + 1) * n], xT[:, c, t * HT:(t + 1) * HT],
                                    w[:, c, col:col + n], start=(c == 0), stop=(c == 1))
                    op.then_inc(full[name], 1)

                def scores0(u):
                    t, m = u // 2, u % 2
                    b = free(f"scores0_{u}")
                    for j in range(3):
                        op = mm(b[0:HT, j * T:(j + 1) * T], q0p[:, j, m, t * HT:(t + 1) * HT], k0[:, m, :],
                                start=True, stop=True)
                    op.then_inc(full[f"scores0_{u}"], 1)

                def scores1(u):
                    b = free(f"scores1_{u}")
                    mm(b[0:HT, 0:492], ident_bf[:, :], mask_bf[:, 0 if u < 2 else 1, :], start=True, stop=False)
                    if u < 2:
                        for j in range(6):
                            op = mm(b[0:HT, j * HT:(j + 1) * HT], q1p[:, j, u, 0:HT], k1[:, u, 0:HT],
                                    start=False, stop=(j == 5))
                    else:
                        for j in range(3):
                            hd = 3 * (u - 2) + j
                            op = mm(b[0:HT, j * T:(j + 1) * T], q1p[:, hd % 6, hd // 6, HT:T], k1[:, hd // 6, :],
                                    start=False, stop=(j == 2))
                    op.then_inc(full[f"scores1_{u}"], 1)

                def probs0(u):
                    kt, m = u // 2, u % 2
                    b = free(f"probs0T_{u}")
                    pe.wait_ge(p0_by_pool if m else p0_by_dve, 2 * i + 2)
                    for j in range(3):
                        for t in range(2):
                            op = tr(b[0:HT, j * T + t * HT:j * T + (t + 1) * HT],
                                    p0[:, t, 3 * m + j, kt * HT:(kt + 1) * HT], ident[0:HT, 0:HT])
                    op.then_inc(full[f"probs0T_{u}"], 1)

                def probs1(u):
                    b = free(f"probs1T_{u}")
                    for s, k in {0: ((p1_by_dve, 2),), 1: ((p1_by_dve, 1), (p1_by_pool, 2)),
                                 2: ((p1_by_pool, 1), (p1_by_dve, 3)), 3: ((p1_by_pool, 1), (p1_by_dve, 4)),
                                 4: ((p1_by_dve, 2), (p1_by_pool, 2)), 5: ((p1_by_dve, 4),)}[u]:
                        pe.wait_ge(s, (4 if s is p1_by_dve else 2) * (i - 1) + k)
                    if u < 4:
                        for j in range(3):
                            hd = 3 * u + j
                            tr(b[0:HT, j * T:j * T + HT], p1a[:, hd, :], ident[0:HT, 0:HT])
                            op = tr(b[0:HT, j * T + HT:(j + 1) * T], p1b[:, hd, 0:HT], ident[0:HT, 0:HT])
                    else:
                        for j in range(6):
                            hd = 6 * (u - 4) + j
                            op = tr(b[0:HT, j * HT:(j + 1) * HT], p1b[:, hd, HT:T], ident[0:HT, 0:HT])
                    op.then_inc(full[f"probs1T_{u}"], 1)

                def weigh0():
                    b = free("att0")
                    for m in range(2):
                        for kt in range(2):
                            have(pe, f"probs0T_{2 * kt + m}", i)
                            for r in range(3):
                                hd = 3 * m + r
                                op = mm(b[32 * r:32 * r + 32, m * T:(m + 1) * T], v0[:, kt, 32 * hd:32 * hd + 32],
                                        p0T[:, kt, hd, :], start=(kt == 0), stop=(kt == 1))
                    op.then_inc(full["att0"], 1)

                def weigh1(m):
                    b = free("att1") if m == 0 else bank_of("att1")
                    have(pe, f"probs1T_{2 * m}", i)
                    have(pe, f"probs1T_{2 * m + 1}", i)
                    for odd in range(2):
                        for r in range(3):
                            hd = 6 * m + 2 * r + odd
                            mm(b[32 * r:32 * r + 32, m * T:(m + 1) * T], v1[:, 0, hd, :], p1aT[:, hd, :],
                               start=(odd == 0), stop=False)
                    have(pe, f"probs1T_{4 + m}", i)
                    for odd in range(2):
                        for r in range(3):
                            hd = 6 * m + 2 * r + odd
                            op = mm(b[32 * r:32 * r + 32, m * T + HT:(m + 1) * T], v1[:, 1, hd, :], p1bT[:, hd, :],
                                    start=False, stop=(odd == 1))
                    if m == 1:
                        op.then_inc(full["att1"], 1)

                if isinstance(i, int) and i == 0:
                    pe.wait_ge(x_made[0], 1)
                    turn("x1T", x1, bank_of("x1T"))
                    embed(PART[2] + 1)
                    pe.wait_ge(weights_in, 16 * N_WEIGHTS)
                    pe.wait_ge(taken["x1T"], 1)
                    stationary("q0", wq_s, 0, x1T, bank[0])
                    stationary("k0", wk_s, 0, x1T, bank[1])
                if l0:
                    wait(pe, taken["q0"], i + 1)
                    wait(pe, taken["k0"], i + 1)
                    for u in range(3):
                        scores0(u)
                if l1:
                    pe.wait_ge(x_made[2], i)
                    turn("x3T", x3)
                if l0:
                    scores0(3)
                if isinstance(i, int) and i == 0:
                    for n in range(PART[2] + 2, NPT):
                        embed(n)
                    moving("v0", wv_s, 0, x1T, b=bank_of("v0"))
                    pe.wait_ge(tok_taken, NPT)
                if l1:
                    have(pe, "x3T", i)
                    stationary("q1", w_attn_s, 0, x3T)
                    stationary("k1", w_attn_s, D, x3T)
                    moving("v1", w_attn_s, 2 * D, x3T)
                    pe.wait_ge(q1p_made, 3 * i)
                    have(pe, "k1", i)
                if l1:
                    scores1(S1_ORDER[0])
                    scores1(S1_ORDER[1])
                for n in range(4):
                    if l0:
                        probs0(P0_ORDER[n])
                    if l1:
                        scores1(S1_ORDER[2 + n])
                if l0:
                    wait(pe, taken["v0"], i + 1)
                    weigh0()
                if l1:
                    probs1(P1_ORDER[0])
                    probs1(P1_ORDER[1])
                if ahead:
                    pe.wait_ge(x_made[0], i + 2)
                    turn("x1T", x1)
                if l0:
                    have(pe, "att0", i)
                    b = free("proj0")
                    for t in range(2):
                        for m in range(2):
                            op = mm(b[0:HT, t * D:(t + 1) * D], att0[:, m * T + t * HT:m * T + (t + 1) * HT],
                                    wo_s[:, m, :], start=(m == 0), stop=(m == 1))
                    op.then_inc(full["proj0"], 1)
                if l1:
                    probs1(P1_ORDER[2])
                    probs1(P1_ORDER[3])
                    have(pe, "v1", i)
                    weigh1(0)
                    probs1(P1_ORDER[4])
                    probs1(P1_ORDER[5])
                if ahead:
                    have(pe, "x1T", i)
                    stationary("k0", wk_s, 0, x1T)
                if l1:
                    weigh1(1)
                if l0:
                    pe.wait_ge(x_made[1], i + 1)
                    turn("x2T", x2)
                if ahead:
                    stationary("q0", wq_s, 0, x1T)
                if l1:
                    have(pe, "att1", i)
                    b = free("proj1")
                    for t in range(2):
                        for m in range(2):
                            op = mm(b[0:HT, t * D:(t + 1) * D], att1[:, m * T + t * HT:m * T + (t + 1) * HT],
                                    w_proj_s[:, m, :], start=(m == 0), stop=(m == 1))
                    op.then_inc(full["proj1"], 1)
                if l0:
                    have(pe, "x2T", i)
                    for half, name in enumerate(("hid_a", "hid_b")):
                        b = free(name)
                        for j in range(3):
                            m = 3 * half + j
                            for c in range(2):
                                op = mm(b[:, j * T:(j + 1) * T], ffn_in_s[:, c, m * 128:(m + 1) * 128],
                                        x2T[:, c, :], start=(c == 0), stop=(c == 1))
                        op.then_inc(full[name], 1)
                if l0:
                    b = free("ffn")
                    have(pe, "hid_a", i)
                for t in range(2):
                    for m in range(FM):
                        if t == 0 and m == 3:
                            if l1:
                                pe.wait_ge(x_made[3], i)
                                turn("x4T", x4)
                            if l0:
                                have(pe, "hid_b", i)
                        if l0:
                            op = mm(b[0:HT, t * D:(t + 1) * D], hid[:, m, t * HT:(t + 1) * HT],
                                    ffn_out_s[:, m, :], start=(m == 0), stop=(m == FM - 1))
                if l0:
                    op.then_inc(full["ffn"], 1)
                if ahead:
                    moving("v0", wv_s, 0, x1T)
                if l1:
                    have(pe, "x4T", i)
                    moving("logits", w_router_s, 0, x4T, n=E)

            def route_first():
                pe.wait_ge(taken[f"probs1T_{P1_ORDER[4]}"], rounds(f"probs1T_{P1_ORDER[4]}", B - 1))
                route_places(pe, [bank_of(f"probs1T_{P1_ORDER[4]}")], 0, 1, 0)

            batch_loop(pe, body, route_first)

        @blk.vector
        def _(dve):
            V = nc.vector
            dve.wait_ge(patches_in[0], 64)
            V.tensor_tensor(tok_bias_s, tok_bias_s, tok_b_s, ALU.add).then_inc(vec_setup, 1)
            dve.wait_ge(vec_setup, 1)

            def embed(n):
                m = min(PB, B * NPATCH - n * PB)
                dve.wait_ge(tok_full, n + 1)
                V.tensor_tensor(emb[0:m, n, :], embed_bank(n)[0:m, 0:D], tok_bias_s[0:m, :],
                                ALU.add).then_inc(tok_taken, 1)

            for n in range(PART[1]):
                embed(n)
            dve.wait_ge(consts_in, CONSTS)
            V.tensor_copy(mask_bf[:, :, :].rearrange("p a b -> p (a b)"),
                          con[0:HT, C_MASK_A:C_MASK_A + 984]).then_inc(vec_setup, 1)

            def norm_stats(n, b, made):
                for t in range(2):
                    op = V.bn_stats(stats[n][:, t, :], tile1(b, t).rearrange("p a d -> p (a d)"))
                op.then_inc(made, 1)

            def norm_var(n, made, made_count, count):
                wait_apart(dve, made, made_count)
                for t in range(2):
                    op = V.bn_aggr(mv[n][:, t, :], stats[n][:, t, :])
                op.then_inc(mv_made[n], 1)
                dve.wait_ge(mv_made[n], count)
                V.tensor_scalar(var_eps[n], mv[n][:, :, 1], EPS, None, ALU.add).then_inc(var_made[n], 1)

            def norm_apply(n, b, count):
                dve.wait_ge(rstd_made[n], count)
                for t in range(2):
                    op = V.tensor_scalar(XN[n][:, t, :], tile1(b, t).rearrange("p a d -> p (a d)"),
                                         mv[n][:, t, 0:1], rstd[n][:, t:t + 1], ALU.subtract, ALU.mult)
                op.then_inc(x_made[n], 1)

            def top0(u, i):
                t, m = u // 2, u % 2
                need(dve, f"scores0_{u}", i)
                V.tensor_reduce(nmax0[:, t, 3 * m:3 * m + 3],
                                bank_of(f"scores0_{u}")[0:HT, 0:3 * T].rearrange("p (h k) -> p h k", h=3),
                                AX.X, ALU.max, negate=True).then_inc(nmax0_made, 1)

            def top1(u, i):
                need(dve, f"scores1_{u}", i)
                o, n = (nmax1[:, 0, 6 * u:6 * u + 6], 6) if u < 2 else (nmax1[:, 1, 3 * u - 6:3 * u - 3], 3)
                V.tensor_reduce(o, bank_of(f"scores1_{u}")[0:HT, 0:492].rearrange("p (h k) -> p h k", h=n),
                                AX.X, ALU.max, negate=True).then_inc(nmax1_made, 1)

            def invert0(u, i):
                t, m = u // 2, u % 2
                have(dve, f"scores0_{u}", i)
                V.reciprocal(inv0[:, t, 3 * m:3 * m + 3], sum0[:, t, 3 * m:3 * m + 3]).then_inc(inv0_made, 1)

            def invert1(u, i):
                have(dve, f"scores1_{u}", i)
                t, heads = (0, slice(6 * u, 6 * u + 6)) if u < 2 else (1, slice(3 * u - 6, 3 * u - 3))
                V.reciprocal(inv1[:, t, heads], sum1[:, t, heads]).then_inc(inv1_made, 1)

            def over_sum0(u, i):
                dve.wait_ge(inv0_made, 4 * i + u + 1)
                rows, inv = p0_rows(u)
                V.tensor_tensor(rows, rows, inv, ALU.mult).then_inc(p0_by_dve, 1)

            def over_sum1(u, i):
                dve.wait_ge(inv1_made, 6 * i - 6 + S1_ORDER.index(u) + 1)
                rows, inv = p1_rows(u)
                V.tensor_tensor(rows, rows, inv, ALU.mult).then_inc(p1_by_dve, 1)

            def take_probs0(u, i):
                need(dve, f"probs0T_{u}", i)
                V.tensor_copy(p0T_unit(u), bank_of(f"probs0T_{u}")[0:HT, 0:492]).then_inc(taken[f"probs0T_{u}"], 1)

            def take_probs1(u, i):
                need(dve, f"probs1T_{u}", i)
                V.tensor_copy(p1T_unit(u), bank_of(f"probs1T_{u}")[0:HT, 0:492]).then_inc(taken[f"probs1T_{u}"], 1)

            for n in range(PART[1], PART[2] - 1):
                embed(n)
            dve.wait_ge(h_emb[0], 48)
            norm_stats(0, 0, first_stats_made)
            norm_var(0, first_stats_made, 1, 1)
            norm_apply(0, 0, 1)
            for n in range(PART[2] - 1, PART[2] + 1):
                embed(n)
            dve.wait_ge(weights_in, 16 * N_WEIGHTS)
            V.tensor_tensor(anchor_p, anchor_w_s, anchors_s, ALU.mult).then_inc(vec_setup, 1)
            dve.wait_ge(vec_setup, 3)
            V.tensor_reduce(anchor_h, anchor_p, AX.X, ALU.add).then_inc(vec_setup, 1)
            dve.wait_ge(vec_setup, 4)
            V.scalar_tensor_tensor(out=k_shift, in0=anchor_h, scalar=float(HD0) ** 0.5,
                                   in1=lam_s, op0=ALU.mult, op1=ALU.mult).then_inc(vec_setup, 1)
            dve.wait_ge(vec_setup, 5)
            embed(PART[2] + 1)

            def take_k0(i, b):
                need(dve, "k0", i)
                V.tensor_tensor(k0, b[0:DH, 0:2 * T].rearrange("p (m t) -> p m t", m=2),
                                k_shift.unsqueeze(2).to_broadcast([DH, 2, T]),
                                ALU.add).then_inc(taken["k0"], 1)

            take_k0(-1, bank[1])

            def body(i, l0, l1, ahead):
                if isinstance(i, int) and i == 1:
                    dve.wait_ge(h_emb[1], 96)
                    dve.wait_ge(text_in, 96)
                if l0:
                    top0(0, i)
                if l1:
                    norm_apply(2, i - 1, i)
                if l0:
                    top0(1, i)
                if l1:
                    need(dve, "x3T", i)
                    V.tensor_copy(x3T.rearrange("p c t -> p (c t)"), bank_of("x3T")[0:DH, 0:2 * T]).then_inc(taken["x3T"], 1)
                if isinstance(i, int) and i == B:
                    route_end(dve, [bank_of(f"probs1T_{P1_ORDER[4]}")], 0, 1, 0, 0)
                if l0:
                    top0(2, i)
                    top0(3, i)
                    invert0(0, i)
                    invert0(1, i)
                    over_sum0(0, i)
                if isinstance(i, int) and i == 0:
                    for n in range(PART[2] + 2, NPT):
                        embed(n)
                if l1:
                    need(dve, "q1", i)
                    V.tensor_tensor(q1b, bank_of("q1")[0:DH, 0:2 * T].rearrange("p (m t) -> p m t", m=2),
                                    qk_bias_s[:, 0, :].unsqueeze(2).to_broadcast([DH, 2, T]),
                                    ALU.add).then_inc(taken["q1"], 1)
                    have(dve, "q1", i)
                    for j in range(3, 6):
                        op = V.tensor_scalar(q1p[:, j, :, :], q1b, con[0:DH, C_QM1 + j:C_QM1 + j + 1], None, ALU.mult)
                    op.then_inc(q1p_made, 1)
                if l1:
                    need(dve, "k1", i)
                    V.tensor_tensor(k1, bank_of("k1")[0:DH, 0:2 * T].rearrange("p (m t) -> p m t", m=2),
                                    qk_bias_s[:, 1, :].unsqueeze(2).to_broadcast([DH, 2, T]),
                                    ALU.add).then_inc(taken["k1"], 1)
                if l0:
                    invert0(2, i)
                    invert0(3, i)
                    over_sum0(2, i)
                if l1:
                    need(dve, "v1", i)
                    for t in range(2):
                        for odd in range(2):
                            mine = "p (h two d) -> p h two d"
                            op = V.tensor_tensor(
                                v1[:, t, odd:H1:2, odd * HD1:(odd + 1) * HD1],
                                bank_of("v1")[0:HT, t * D:(t + 1) * D].rearrange(mine, two=2, d=HD1)[:, :, odd, :],
                                v_bias_s.rearrange(mine, two=2, d=HD1)[:, :, odd, :], ALU.add)
                    op.then_inc(taken["v1"], 1)
                if l1:
                    top1(0, i)
                if ahead:
                    norm_stats(0, i + 1, stats_made[0])
                if l1:
                    top1(2, i)
                if isinstance(i, int) and i == B:
                    group_apply(dve, 0)
                if l0:
                    take_probs0(P0_ORDER[0], i)
                if ahead:
                    norm_var(0, stats_made[0], i + 1, i + 2)
                if l1:
                    invert1(0, i)
                    top1(1, i)
                    over_sum1(0, i)
                if l0:
                    take_probs0(P0_ORDER[1], i)
                if l1:
                    invert1(2, i)
                    top1(3, i)
                if ahead:
                    norm_apply(0, i + 1, i + 2)
                if l1:
                    over_sum1(2, i)
                    invert1(1, i)
                    top1(4, i)
                    invert1(3, i)
                if l0:
                    take_probs0(P0_ORDER[3], i)
                if l1:
                    top1(5, i)
                    invert1(4, i)
                if l0:
                    need(dve, "att0", i)
                    V.tensor_copy(att0, bank_of("att0")[0:DH, 0:2 * T]).then_inc(taken["att0"], 1)
                if l1:
                    over_sum1(4, i)
                    invert1(5, i)
                    over_sum1(5, i)
                    take_probs1(P1_ORDER[1], i)
                if l0:
                    need(dve, "proj0", i)
                    V.tensor_tensor(tile2(i), bank_of("proj0")[0:HT, 0:2 * D].rearrange("p (t d) -> p t d", t=2),
                                    tile2(i), ALU.add).then_inc(taken["proj0"], 1)
                    wait_apart(dve, taken["proj0"], rounds("proj0", i))
                    norm_stats(1, i, stats_made[1])
                if l1:
                    take_probs1(P1_ORDER[3], i)
                if l0:
                    norm_var(1, stats_made[1], i + 1, i + 1)
                if l1:
                    take_probs1(P1_ORDER[5], i)
                if l0:
                    norm_apply(1, i, i + 1)
                if ahead:
                    take_k0(i, bank_of("k0"))
                if isinstance(i, int) and i == B - 1:
                    dve.wait_ge(taken["logits"], B - 2)
                    route_start(dve, 0, 1, 0, 0)
                if l1:
                    need(dve, "proj1", i)
                    wait(dve, proj_bias_added, i)
                    V.tensor_tensor(tile2(i - 1), bank_of("proj1")[0:HT, 0:2 * D].rearrange("p (t d) -> p t d", t=2),
                                    tile2(i - 1), ALU.add).then_inc(taken["proj1"], 1)
                    wait_apart(dve, taken["proj1"], rounds("proj1", i))
                    norm_stats(3, i - 1, stats_made[3])
                    norm_var(3, stats_made[3], i, i)
                    norm_apply(3, i - 1, i)
                if isinstance(i, int) and i == B - 1:
                    route_second(dve, 0, 1, 0)
                    group_stats(dve, 0, xg_first_stats, 1)
                if l0:
                    need(dve, "ffn", i)
                    V.tensor_tensor(tile2(i), bank_of("ffn")[0:HT, 0:2 * D].rearrange("p (t d) -> p t d", t=2),
                                    tile2(i), ALU.add).then_inc(taken["ffn"], 1)
                    wait_apart(dve, taken["ffn"], rounds("ffn", i))
                    norm_stats(2, i, stats_made[2])
                    norm_var(2, stats_made[2], i + 1, i + 1)
                if l1:
                    need(dve, "logits", i)
                    lt = logits[:, bass.ds(2 * i - 2, 2), :] if not isinstance(i, int) else logits[:, 2 * i - 2:2 * i, :]
                    V.tensor_scalar(lt, bank_of("logits")[0:HT, 0:2 * E].rearrange("p (t e) -> p t e", t=2),
                                    1.0, None, ALU.mult).then_inc(taken["logits"], 1)

            batch_loop(dve, body)

        @blk.scalar
        def _(act):
            A = nc.scalar.activation
            act.wait_ge(consts_in, CONSTS)
            A(ident_bf[:, :], ident[0:HT, 0:HT], ACT.Copy).then_inc(act_setup, 1)

            def take(name, dst, parts, cols, i):
                need(act, name, i)
                A(dst, bank_of(name)[0:parts, 0:cols], ACT.Copy).then_inc(taken[name], 1)

            act.wait_ge(full["x1T"], 1)
            A(x1T.rearrange("p c t -> p (c t)"), bank_of("x1T")[0:DH, 0:2 * T], ACT.Copy).then_inc(taken["x1T"], 1)

            def take_q0(i, b):
                need(act, "q0", i)
                for j in range(3):
                    op = A(q0p[:, j, :, :].rearrange("p m t -> p (m t)"), b[0:DH, 0:2 * T], ACT.Copy,
                           scale=con[0:DH, C_QM0 + j:C_QM0 + j + 1])
                op.then_inc(taken["q0"], 1)

            take_q0(-1, bank[0])
            act.wait_ge(weights_in, 16 * N_WEIGHTS)

            def exps0(u, i):
                t, m = u // 2, u % 2
                act.wait_ge(nmax0_made, 4 * i + u + 1)
                for j in range(3):
                    hd = 3 * m + j
                    op = A(p0[:, t, hd, :], bank_of(f"scores0_{u}")[0:HT, j * T:(j + 1) * T], ACT.Exp,
                           bias=nmax0[:, t, hd:hd + 1], accum_out=sum0[:, t, hd:hd + 1])
                op.then_inc(taken[f"scores0_{u}"], 1)

            def exps1(u, i):
                act.wait_ge(nmax1_made, 6 * i - 6 + S1_ORDER.index(u) + 1)
                t, dst, n, w, first = (0, p1a, 6, HT, 6 * u) if u < 2 else (1, p1b, 3, T, 3 * u - 6)
                for j in range(n):
                    hd = first + j
                    op = A(dst[:, hd, :], bank_of(f"scores1_{u}")[0:HT, j * w:(j + 1) * w], ACT.Exp,
                           bias=nmax1[:, t, hd:hd + 1], accum_out=sum1[:, t, hd:hd + 1])
                op.then_inc(taken[f"scores1_{u}"], 1)

            def body(i, l0, l1, ahead):
                if l0:
                    for u in range(4):
                        exps0(u, i)
                if isinstance(i, int) and i == 0:
                    act.wait_ge(full["v0"], 1)
                    A(v0.rearrange("p t d -> p (t d)"), bank_of("v0")[0:HT, 0:2 * D], ACT.Copy).then_inc(taken["v0"], 1)
                if l1:
                    have(act, "q1", i)
                    for j in range(2):
                        op = A(q1p[:, j, :, :], q1b, ACT.Copy, scale=con[0:DH, C_QM1 + j:C_QM1 + j + 1])
                    op.then_inc(q1p_made, 1)
                    exps1(S1_ORDER[0], i)
                    exps1(S1_ORDER[1], i)
                for n in range(4):
                    if l0 and n == 2:
                        u = P0_ORDER[n]
                        take(f"probs0T_{u}", p0T_unit(u), HT, 492, i)
                    if l1:
                        exps1(S1_ORDER[2 + n], i)
                if l1:
                    take(f"probs1T_{P1_ORDER[0]}", p1T_unit(P1_ORDER[0]), HT, 492, i)
                if ahead:
                    take("x1T", x1T.rearrange("p c t -> p (c t)"), DH, 2 * T, i)
                if l1:
                    for u in P1_ORDER[2::2]:
                        take(f"probs1T_{u}", p1T_unit(u), HT, 492, i)
                    take("att1", att1, DH, 2 * T, i)
                if l0:
                    take("x2T", x2T.rearrange("p c t -> p (c t)"), DH, 2 * T, i)
                if isinstance(i, int) and i == B - 1:
                    route_exps(act, 0, 1, 0)
                if ahead:
                    take_q0(i, bank_of("q0"))
                if isinstance(i, int) and i == 0:
                    act.wait_ge(tok_full, NPT)
                    act.wait_ge(h_emb[1], 96)
                if l0:
                    for half, name in enumerate(("hid_a", "hid_b")):
                        need(act, name, i)
                        for j in range(3):
                            m = 3 * half + j
                            op = A(hid[:, m, :], bank_of(name)[:, j * T:(j + 1) * T], ACT.Gelu,
                                   bias=ffn_bias_s[:, m:m + 1])
                        op.then_inc(taken[name], 1)
                if l1:
                    take("x4T", x4T.rearrange("p c t -> p (c t)"), DH, 2 * T, i)
                if ahead:
                    take("v0", v0.rearrange("p t d -> p (t d)"), HT, 2 * D, i)

            batch_loop(act, body)

    def group_loop(eng, body):
        body(0, True, False)
        with eng.Fori(1, G - 1) as g:
            body(g, True, True)
        body(G - 1, False, True)

    with nc.Block() as blk:
        @blk.sync
        def _(sp):
            def load(g, e):
                n = 8 * g + e
                wait(sp, turned, n - 1)
                rows = slots_in.rearrange("(n t p) d -> n p t d", t=2, p=CT)
                src = rows[n] if isinstance(n, int) else rows[bass.ds(n, 1)].rearrange("a p t d -> (a p) t d")
                sp.dma_start(xin[e % 2], src).then_inc(xin_in[e % 2], 16)

            out_rows = out.rearrange("b (t p) d -> (b t) p d", p=HT).rearrange("(g t) p d -> g p t d", t=GT)

            def store(g):
                dst = out_rows[g] if isinstance(g, int) else out_rows[bass.ds(g, 1)].rearrange("a p t d -> (a p) t d")
                for half in range(2):
                    tiles = slice(HALF_GT * half, HALF_GT * (half + 1))
                    sp.wait_ge(combined, 2 * g + half + 1)
                    sp.dma_start(dst[:, tiles, :], out_g[:, tiles, :]).then_inc(out_stored, 16)

            def body(g, ahead, behind):
                sp.wait_ge(scattered, 256 * g + 256)
                for e in range(E):
                    load(g, e)
                    if not behind:
                        for n in {1: (1, 2), 2: (3,), 3: (4,), 4: (5,), 5: (6,), 6: (7,)}.get(e, ()):
                            load_expert(sp, n)
                if behind:
                    store(g - 1)

            group_loop(sp, body)
            store(G - 1)
            sp.wait_ge(out_stored, 32 * G)

        @blk.gpsimd
        def _(pool):
            P = nc.gpsimd

            def gather(g):
                for n in range(2):
                    wait(pool, y_out[n], 64 * g + 64)
                wait(pool, combined, 2 * g)
                src = from_slot[:, g, :] if isinstance(g, int) else from_slot[:, bass.ds(g, 1), :].rearrange("p a n -> p (a n)")
                P.tensor_copy(from_slot_g[:, :], src).then_inc(from_copied, 1)
                wait_apart(pool, from_copied, g + 1)
                for half in range(2):
                    for k in range(TOPK):
                        for t in range(HALF_GT * half, HALF_GT * (half + 1)):
                            n = k * GT + t
                            P.indirect_dma_start(
                                out=yg[:, n, :], out_offset=None, in_=slots_out,
                                in_offset=bass.IndirectOffsetOnAxis(ap=from_slot_g[:, n:n + 1], axis=0),
                                bounds_check=ALL_SLOTS - 1, oob_is_err=False).then_inc(gathered[half], 16)

            pool.wait_ge(routed, ROUTED)

            def body(g, ahead, behind):
                if ahead:
                    scatter_ready(pool, g + 1)
                    scatter(pool, g + 1)
                if behind:
                    gather(g - 1)

            group_loop(pool, body)
            gather(G - 1)

        @blk.tensor
        def _(pe):
            mm, tr = nc.tensor.matmul, nc.tensor.transpose

            def turn(g, e):
                n = 8 * g + e
                pe.wait_ge(xin_in[e % 2], 64 * g + 16 * (e // 2) + 16)
                wait(pe, turn_taken, n)
                for c in range(2):
                    for t in range(2):
                        op = tr(turn_bank[0:DH, c * SLOTS + t * CT:c * SLOTS + (t + 1) * CT],
                                xin[e % 2][:, t, c * DH:(c + 1) * DH], ident[0:CT, 0:CT])
                op.then_inc(turned, 1)

            def up(g, e):
                n = 8 * g + e
                pe.wait_ge(moe_in[e], 32 if e < 2 else 64)
                wait(pe, turn_taken, n + 1)
                for j in range(3):
                    wait(pe, hid_taken, 3 * n - 2 + j)
                    for k in range(2):
                        m = 2 * j + k
                        for c in range(2):
                            op = mm(hid_banks[j][:, k * SLOTS:(k + 1) * SLOTS], wi_s[e][:, c, m * 128:(m + 1) * 128],
                                    xinT[e % 2][:, c, :], start=(c == 0), stop=(c == 1))
                    op.then_inc(hid_full, 1)

            def down(g, e):
                n = 8 * g + e
                wait(pe, hid_taken, 3 * n + 3)
                wait(pe, y_taken, n - 1)
                for t in range(2):
                    for m in range(FM):
                        op = mm(y_banks[e % 2][0:CT, t * D:(t + 1) * D], hidT[e % 2][:, m, t * CT:(t + 1) * CT],
                                wo_moe_s[e][:, m, :], start=(m == 0), stop=(m == FM - 1))
                op.then_inc(y_full, 1)

            def after(g, e, k):
                return (g, e + k) if e + k < E else (g + 1, e + k - E)

            turn(0, 0)
            turn(0, 1)
            up(0, 0)

            def body(g, ahead, behind):
                for e in range(E):
                    if ahead or e + 2 < E:
                        turn(*after(g, e, 2))
                    if ahead or e + 1 < E:
                        up(*after(g, e, 1))
                    down(g, e)
                    if not behind and e == 0:
                        route_places(pe, place_banks, 1, G, ROUTED_FIRST)

            group_loop(pe, body)

        @blk.vector
        def _(dve):
            V = nc.vector

            route_start(dve, 1, G, ROUTED_FIRST, 1)
            route_second(dve, 1, G, ROUTED_FIRST)
            route_end(dve, place_banks, 1, G, ROUTED_FIRST, 1)

            def combine(g):
                wait(dve, combined, 2 * g)
                V.tensor_copy(gate_g.rearrange("p (k t) -> p k t", k=TOPK),
                              gate[:, g, :, :] if isinstance(g, int) else
                              gate[:, bass.ds(g, 1), :, :].rearrange("p a k t -> p (a k) t")).then_inc(gates_copied, 1)
                dve.wait_ge(gates_copied, g + 1)
                wait(dve, out_stored, 32 * g)
                for half in range(2):
                    dve.wait_ge(gathered[half], 128 * g + 128)
                    tiles = range(HALF_GT * half, HALF_GT * (half + 1))
                    for t in tiles:
                        op = V.scalar_tensor_tensor(out=out_g[:, t, :], in0=yg[:, t, :], scalar=gate_g[:, t:t + 1],
                                                    in1=at(h, 8 * g + t).rearrange("p a d -> p (a d)"),
                                                    op0=ALU.mult, op1=ALU.add)
                    op.then_inc(first_added, 1)
                    dve.wait_ge(first_added, 2 * g + half + 1)
                    for t in tiles:
                        op = V.scalar_tensor_tensor(out=out_g[:, t, :], in0=yg[:, GT + t, :],
                                                    scalar=gate_g[:, GT + t:GT + t + 1], in1=out_g[:, t, :],
                                                    op0=ALU.mult, op1=ALU.add)
                    op.then_inc(combined, 1)

            def body(g, ahead, behind):
                if ahead:
                    group_stats(dve, g + 1, xg_stats, g + 1)
                    group_apply(dve, g + 1)
                if behind:
                    combine(g - 1)

            group_loop(dve, body)
            combine(G - 1)

        @blk.scalar
        def _(act):
            A = nc.scalar.activation
            route_exps(act, 1, G, ROUTED_FIRST)

            def turn(g, e):
                n = 8 * g + e
                act.wait_ge(turned, n + 1)
                A(xinT[e % 2].rearrange("p c s -> p (c s)"), turn_bank[0:DH, 0:2 * SLOTS], ACT.Copy).then_inc(turn_taken, 1)

            def up(g, e):
                n = 8 * g + e
                for j in range(3):
                    act.wait_ge(hid_full, 3 * n + j + 1)
                    A(hidT[e % 2][:, 2 * j:2 * j + 2, :].rearrange("p m s -> p (m s)"),
                      hid_banks[j][:, 0:2 * SLOTS], ACT.Relu).then_inc(hid_taken, 1)

            rows = slots_out.rearrange("(n t p) d -> n p t d", t=2, p=CT)

            def down(g, e):
                n = 8 * g + e
                act.wait_ge(y_full, n + 1)
                wait(act, y_out[e % 2], 64 * g + 16 * (e // 2))
                A(y[e % 2].rearrange("p t d -> p (t d)"), y_banks[e % 2][0:CT, 0:2 * D], ACT.Copy).then_inc(y_taken, 1)
                act.wait_ge(y_taken, n + 1)
                dst = rows[n] if isinstance(n, int) else rows[bass.ds(n, 1)].rearrange("a p t d -> (a p) t d")
                act.dma_start(dst, y[e % 2]).then_inc(y_out[e % 2], 16)

            def after(g, e, k):
                return (g, e + k) if e + k < E else (g + 1, e + k - E)

            turn(0, 0)
            turn(0, 1)
            up(0, 0)

            def body(g, ahead, behind):
                for e in range(E):
                    if ahead or e + 2 < E:
                        turn(*after(g, e, 2))
                    if ahead or e + 1 < E:
                        up(*after(g, e, 1))
                    down(g, e)

            group_loop(act, body)
            for n in range(2):
                act.wait_ge(y_out[n], 64 * G)


R_START = 13
R_BEFORE = R_START + 11
ROUTED_FIRST = R_BEFORE + 13
ROUTED = ROUTED_FIRST + R_BEFORE + 14
HALF_GT = GT // 2
GCOLS = E * TOPK * GT


def constants():
    import numpy as np
    c = np.zeros((128, C_ALL), np.float32)
    p = np.arange(128)
    c[:, C_IDENT:C_IDENT + 128] = np.eye(128)
    c[:, C_ONES:C_ONES + 128] = 1.0
    for j in range(3):
        c[(p // HD0) == j, C_QM0 + j] = HD0 ** -0.5
    for j in range(6):
        c[(p // HD1) == j, C_QM1 + j] = HD1 ** -0.5
    causal = np.where(np.arange(HT)[None, :] <= p[:, None], 0.0, MASKED)
    c[:, C_MASK_A:C_MASK_A + 492] = np.tile(causal, (1, 6))
    c[:, C_MASK_B:C_MASK_B + 492] = np.tile(np.concatenate([np.zeros((128, HT)), causal], 1), (1, 3))
    c[:, C_TRI:C_TRI + HT] = p[:, None] < np.arange(HT)[None, :]
    c[:, C_REV:C_REV + E] = E - np.arange(E)
    c[:, C_RESET:C_RESET + 1024] = np.arange(1024) % (TOPK * GT) != 0
    c[:, C_BASE:C_BASE + 128] = np.repeat(np.arange(G) * GROUP_SLOTS, TOPK * GT)
    c[:, C_HALF:C_HALF + 8] = -0.5
    return c


def kernel(x, txt, L0_tok_W, L0_tok_b, L0_tok_pos_embed, L0_attn_Wq, L0_attn_Wk, L0_attn_Wv, L0_attn_Wo,
           L0_attn_anchor_w, L0_attn_anchors, L0_attn_lam, L0_ffn_in_weight, L0_ffn_in_bias, L0_ffn_out_weight,
           L1_attn_w_attn, L1_attn_b_attn, L1_attn_w_proj, L1_attn_b_proj, L1_ffn_w_router, L1_ffn_wi, L1_ffn_wo):
    import numpy as np
    import concourse.bacc as bacc
    from concourse.bass_utils import run_bass_kernel_spmd

    def rows(a, n):
        return np.broadcast_to(np.asarray(a), (n,) + np.shape(a))

    def halves(a):
        a = np.asarray(a)
        return np.moveaxis(a.reshape((2, DH) + a.shape[1:]), 0, 1)

    patches = np.asarray(x).reshape(B, 3, 6, 16, 6, 16).transpose(1, 3, 5, 0, 2, 4).reshape(PATCH_DIM, B * NPATCH)
    b_attn = np.asarray(L1_attn_b_attn)
    arrays = {
        "patchesT": patches,
        "txt": txt,
        "tok_w": np.asarray(L0_tok_W).T,
        "tok_bias": np.tile(np.asarray(L0_tok_pos_embed)[0], (3, 1)),
        "tok_b": rows(L0_tok_b, PB),
        "wq": np.asarray(L0_attn_Wq).T,
        "wk": np.asarray(L0_attn_Wk).T,
        "wv": np.asarray(L0_attn_Wv).T,
        "wo": np.asarray(L0_attn_Wo).T,
        "anchor_w": halves(np.asarray(L0_attn_anchor_w).reshape(D, 6)),
        "anchors": halves(np.repeat(np.asarray(L0_attn_anchors), HD0, 0)),
        "lam": halves(np.repeat(np.asarray(L0_attn_lam), HD0)),
        "ffn_in": np.asarray(L0_ffn_in_weight).T,
        "ffn_bias": np.asarray(L0_ffn_in_bias).reshape(FM, 128).T,
        "ffn_out": L0_ffn_out_weight,
        "w_attn": L1_attn_w_attn,
        "qk_bias": np.moveaxis(b_attn[:2 * D].reshape(2, 2, DH), 2, 0),
        "v_bias": rows(b_attn[2 * D:], HT),
        "w_proj": L1_attn_w_proj,
        "proj_bias": rows(rows(L1_attn_b_proj, 2), HT),
        "w_router": L1_ffn_w_router,
        "wi": L1_ffn_wi,
        "wo_moe": L1_ffn_wo,
        "consts": constants(),
    }
    nc = bacc.Bacc("TRN2", target_bir_lowering=False, num_devices=1)
    given, args = {}, {}
    for name, a in arrays.items():
        a = np.ascontiguousarray(a)
        given[f"in_{name}"] = a
        args[name] = nc.dram_tensor(f"in_{name}", a.shape, mybir.dt.from_np(a.dtype), kind="ExternalInput").ap()
    out = nc.dram_tensor("out", (B, T, D), F32, kind="ExternalOutput").ap()
    program(nc, out=out, **args)
    r = run_bass_kernel_spmd(nc, [given], core_ids=[0])
    return r.results[0]["out"]
```
